# Optimizing a Trainium2 kernel written in Bass

```python
import numpy as np
import jax
import jax.numpy as jnp

def _softmax(x, axis=-1):
    return jax.nn.softmax(x, axis=axis)

def _gelu(x):
    return jax.nn.gelu(x, approximate=True)

def _silu(x):
    return jax.nn.silu(x)

def _sigmoid(x):
    return jax.nn.sigmoid(x)

def _layernorm(x, axis=-1, eps=1e-05):
    m = jnp.mean(x, axis=axis, keepdims=True)
    v = jnp.var(x, axis=axis, keepdims=True)
    return (x - m) / jnp.sqrt(v + eps)

def _scatter_add(tgt, idx, src, axis=0):
    return tgt.at[idx].add(src)

def _segment_sum(src, seg, n):
    return jax.ops.segment_sum(src, seg, n)
kernel_name = 'mk_lm_tower_d1_tok_ids1024_r4_3a3f6a'

def setup_inputs(seed: int=0):
    np.random.seed(seed)
    _w = jnp.asarray

    def _rec_inputs():
        import jax
        import jax.numpy as jnp
        _rk = jax.random.key(seed)
        x = jax.random.randint(jax.random.fold_in(_rk, 1), (4, 512), 0, 12564, jnp.int32)
        return x
    x = _rec_inputs()

    def _L0_tok_setup():
        import jax, jax.numpy as jnp
        import numpy as np
        VOCAB = 50257
        D_MODEL = 256
        key = jax.random.key(seed)
        k_ids, k_w = jax.random.split(key)
        token_ids = jax.random.randint(k_ids, (4, 1024), 0, VOCAB, dtype=jnp.int64 if jax.config.jax_enable_x64 else jnp.int32)
        W = jax.random.truncated_normal(k_w, -3.0, 3.0, (VOCAB, D_MODEL), dtype=jnp.float32)
        return {'token_ids': token_ids, 'W': W}
    _L0_tok_all = _L0_tok_setup()
    _L0_tok_in = {k: v for k, v in _L0_tok_all.items() if k in ('W',)}
    del _L0_tok_all

    def _L0_attn_setup():
        import jax, jax.numpy as jnp
        import numpy as np
        DIM = 256
        HEADS = 16
        WINDOW = 128
        LOOK_BACKWARD = 1
        LOOK_FORWARD = 0

        def look_around(x, backward=1, forward=0, pad_value=-1):
            w = x.shape[1]
            pad_width = [(0, 0)] * x.ndim
            pad_width[1] = (backward, forward)
            padded = jnp.pad(x, pad_width, constant_values=pad_value)
            tensors = [padded[:, i:i + w] for i in range(forward + backward + 1)]
            return jnp.concatenate(tensors, axis=2)

        def _local_attn(q, k, v):
            b, h, n, d = q.shape
            ws = WINDOW
            windows = n // ws
            merge = lambda t: t.reshape(b * h, n, d)
            q, k, v = (merge(q), merge(k), merge(v))
            bucket = lambda t: t.reshape(b * h, windows, ws, d)
            bq, bk, bv = (bucket(q), bucket(k), bucket(v))
            bk = look_around(bk, backward=LOOK_BACKWARD, forward=LOOK_FORWARD, pad_value=-1)
            bv = look_around(bv, backward=LOOK_BACKWARD, forward=LOOK_FORWARD, pad_value=-1)
            ticker = jnp.arange(n, dtype=q.dtype).reshape(1, windows, ws)
            bq_t = ticker
            bq_k = look_around(ticker, backward=LOOK_BACKWARD, forward=LOOK_FORWARD, pad_value=-1)
            dots = jnp.einsum('bwie,bwje->bwij', bq, bk) * d ** (-0.5)
            mask_value = -jnp.finfo(dots.dtype).max
            causal_mask = bq_t[:, :, :, None] < bq_k[:, :, None, :]
            pad_mask = bq_k[:, :, None, :] == -1
            dots = jnp.where(causal_mask | pad_mask, mask_value, dots)
            attn = jax.nn.softmax(dots, axis=-1)
            out = jnp.einsum('bwij,bwje->bwie', attn, bv)
            return out.reshape(b, h, n, d)
        key = jax.random.key(seed)
        ks = jax.random.split(key, 9)
        s = 0.02
        return {'x': jax.random.normal(ks[0], (4, 1024, DIM), dtype=jnp.float32), 'Wq': jax.random.normal(ks[1], (DIM, DIM), dtype=jnp.float32) * s, 'bq': jax.random.normal(ks[2], (DIM,), dtype=jnp.float32) * s, 'Wk': jax.random.normal(ks[3], (DIM, DIM), dtype=jnp.float32) * s, 'bk': jax.random.normal(ks[4], (DIM,), dtype=jnp.float32) * s, 'Wv': jax.random.normal(ks[5], (DIM, DIM), dtype=jnp.float32) * s, 'bv': jax.random.normal(ks[6], (DIM,), dtype=jnp.float32) * s, 'Wo': jax.random.normal(ks[7], (DIM, DIM), dtype=jnp.float32) * s, 'bo': jax.random.normal(ks[8], (DIM,), dtype=jnp.float32) * s}
    _L0_attn_all = _L0_attn_setup()
    _L0_attn_in = {k: v for k, v in _L0_attn_all.items() if k in ('Wq', 'bq', 'Wk', 'bk', 'Wv', 'bv', 'Wo', 'bo')}
    del _L0_attn_all

    def _L0_ffn_setup():
        import jax, jax.numpy as jnp
        import numpy as np
        NUM_HEADS = 16
        TOP_K = 2
        key = jax.random.key(seed)
        ks = jax.random.split(key, 5)
        B, S, D, E = (4, 512, 256, 8)
        scale = 0.02
        return {'x': jax.random.normal(ks[0], (B, S, D), dtype=jnp.float32), 'W_qkv': jax.random.normal(ks[1], (D, 3 * D), dtype=jnp.float32) * scale, 'b_qkv': jnp.zeros((3 * D,), dtype=jnp.float32), 'W_gate': jax.random.normal(ks[2], (D, E), dtype=jnp.float32) * scale, 'b_gate': jnp.zeros((E,), dtype=jnp.float32), 'W_experts': jax.random.normal(ks[3], (E, D, D), dtype=jnp.float32) * scale, 'b_experts': jnp.zeros((E, D), dtype=jnp.float32)}
    _L0_ffn_all = _L0_ffn_setup()
    _L0_ffn_in = {k: v for k, v in _L0_ffn_all.items() if k in ('W_qkv', 'b_qkv', 'W_gate', 'b_gate', 'W_experts', 'b_experts')}
    del _L0_ffn_all
    return {'x': x, 'L0_tok_W': _L0_tok_in['W'], 'L0_attn_Wq': _L0_attn_in['Wq'], 'L0_attn_bq': _L0_attn_in['bq'], 'L0_attn_Wk': _L0_attn_in['Wk'], 'L0_attn_bk': _L0_attn_in['bk'], 'L0_attn_Wv': _L0_attn_in['Wv'], 'L0_attn_bv': _L0_attn_in['bv'], 'L0_attn_Wo': _L0_attn_in['Wo'], 'L0_attn_bo': _L0_attn_in['bo'], 'L0_ffn_W_qkv': _L0_ffn_in['W_qkv'], 'L0_ffn_b_qkv': _L0_ffn_in['b_qkv'], 'L0_ffn_W_gate': _L0_ffn_in['W_gate'], 'L0_ffn_b_gate': _L0_ffn_in['b_gate'], 'L0_ffn_W_experts': _L0_ffn_in['W_experts'], 'L0_ffn_b_experts': _L0_ffn_in['b_experts']}

def reference(x, L0_tok_W, L0_attn_Wq, L0_attn_bq, L0_attn_Wk, L0_attn_bk, L0_attn_Wv, L0_attn_bv, L0_attn_Wo, L0_attn_bo, L0_ffn_W_qkv, L0_ffn_b_qkv, L0_ffn_W_gate, L0_ffn_b_gate, L0_ffn_W_experts, L0_ffn_b_experts):
    import jax
    import jax.numpy as jnp

    def _L0_tok_ref(token_ids, W):
        import jax, jax.numpy as jnp
        import numpy as np
        VOCAB = 50257
        D_MODEL = 256
        return jnp.take(W, token_ids, axis=0)

    def _L0_attn_ref(x, Wq, bq, Wk, bk, Wv, bv, Wo, bo):
        import jax, jax.numpy as jnp
        import numpy as np
        DIM = 256
        HEADS = 16
        WINDOW = 128
        LOOK_BACKWARD = 1
        LOOK_FORWARD = 0

        def look_around(x, backward=1, forward=0, pad_value=-1):
            w = x.shape[1]
            pad_width = [(0, 0)] * x.ndim
            pad_width[1] = (backward, forward)
            padded = jnp.pad(x, pad_width, constant_values=pad_value)
            tensors = [padded[:, i:i + w] for i in range(forward + backward + 1)]
            return jnp.concatenate(tensors, axis=2)

        def _local_attn(q, k, v):
            b, h, n, d = q.shape
            ws = WINDOW
            windows = n // ws
            merge = lambda t: t.reshape(b * h, n, d)
            q, k, v = (merge(q), merge(k), merge(v))
            bucket = lambda t: t.reshape(b * h, windows, ws, d)
            bq, bk, bv = (bucket(q), bucket(k), bucket(v))
            bk = look_around(bk, backward=LOOK_BACKWARD, forward=LOOK_FORWARD, pad_value=-1)
            bv = look_around(bv, backward=LOOK_BACKWARD, forward=LOOK_FORWARD, pad_value=-1)
            ticker = jnp.arange(n, dtype=q.dtype).reshape(1, windows, ws)
            bq_t = ticker
            bq_k = look_around(ticker, backward=LOOK_BACKWARD, forward=LOOK_FORWARD, pad_value=-1)
            dots = jnp.einsum('bwie,bwje->bwij', bq, bk) * d ** (-0.5)
            mask_value = -jnp.finfo(dots.dtype).max
            causal_mask = bq_t[:, :, :, None] < bq_k[:, :, None, :]
            pad_mask = bq_k[:, :, None, :] == -1
            dots = jnp.where(causal_mask | pad_mask, mask_value, dots)
            attn = jax.nn.softmax(dots, axis=-1)
            out = jnp.einsum('bwij,bwje->bwie', attn, bv)
            return out.reshape(b, h, n, d)
        b, n, dim = x.shape
        h = HEADS
        d = dim // h
        q = x @ Wq + bq
        k = x @ Wk + bk
        v = x @ Wv + bv
        split = lambda t: t.reshape(b, n, h, d).transpose(0, 2, 1, 3)
        out = _local_attn(split(q), split(k), split(v))
        out = out.transpose(0, 2, 1, 3).reshape(b, n, dim)
        return out @ Wo + bo

    def _L0_ffn_ref(x, W_qkv, b_qkv, W_gate, b_gate, W_experts, b_experts):
        import jax, jax.numpy as jnp
        import numpy as np
        NUM_HEADS = 16
        TOP_K = 2
        B, S, D = x.shape
        H = NUM_HEADS
        hd = D // H
        E = W_gate.shape[-1]
        qkv = (x @ W_qkv + b_qkv).reshape(B, S, 3, H, hd)
        q, k, v = (qkv[:, :, 0], qkv[:, :, 1], qkv[:, :, 2])
        attn = jnp.einsum('bqhd,bkhd->bhqk', q, k) / jnp.sqrt(jnp.asarray(hd, x.dtype))
        attn = jax.nn.softmax(attn, axis=-1)
        attn_out = jnp.einsum('bhqk,bkhd->bqhd', attn, v).reshape(B, S, D)
        gate = jax.nn.softmax(x @ W_gate + b_gate, axis=-1)
        top_g, top_i = jax.lax.top_k(gate, TOP_K)
        combine = jnp.sum(jax.nn.one_hot(top_i, E, dtype=x.dtype) * top_g[..., None], axis=2)
        expert_out = jnp.einsum('bsd,edf->bsef', x, W_experts) + b_experts
        moe_out = jnp.einsum('bsef,bse->bsf', expert_out, combine)
        return attn_out + moe_out
    h = _L0_tok_ref(x, L0_tok_W)
    h = h + _L0_attn_ref(_layernorm(h, axis=-1), L0_attn_Wq, L0_attn_bq, L0_attn_Wk, L0_attn_bk, L0_attn_Wv, L0_attn_bv, L0_attn_Wo, L0_attn_bo)
    h = h + _L0_ffn_ref(_layernorm(h, axis=-1), L0_ffn_W_qkv, L0_ffn_b_qkv, L0_ffn_W_gate, L0_ffn_b_gate, L0_ffn_W_experts, L0_ffn_b_experts)
    return h

_drawn_inputs = setup_inputs


def setup_inputs(seed=0):
    import zlib

    import numpy as np

    out = dict(_drawn_inputs(seed))
    spreads = {'L0_ffn_b_qkv': (0.0, 0.1),
     'L0_ffn_b_gate': (0.0, 0.267),
     'L0_ffn_b_experts': (0.0, 0.324)}
    factors = {'L0_attn_Wq': 8.0,
     'L0_attn_bq': 8.0,
     'L0_attn_Wk': 8.0,
     'L0_attn_bk': 200.0,
     'L0_attn_Wv': 3.829,
     'L0_attn_bv': 6.501,
     'L0_attn_Wo': 3.436,
     'L0_ffn_W_qkv': 3.51,
     'L0_attn_bo': 2.927}
    for name, (base, spread) in spreads.items():
        noise = np.random.default_rng([zlib.crc32(name.encode()), seed]).standard_normal(out[name].shape)
        drawn = base * np.exp(spread * noise) if base else spread * noise
        out[name] = jnp.asarray(drawn.astype(out[name].dtype))
    for name, factor in factors.items():
        out[name] = (out[name] * factor).astype(out[name].dtype)
    return out
```

```python
from contextlib import ExitStack

import numpy as np

import concourse.bass as bass
from concourse import mybir

F32 = mybir.dt.float32
BF16 = mybir.dt.bfloat16
I32 = mybir.dt.int32
U32 = mybir.dt.uint32
ALU = mybir.AluOpType
ACT = mybir.ActivationFunctionType
AX = mybir.AxisListType

P = 128
B = 4
T = 512
NT = T // P
D = 256
NC = D // P
H = 16
HD = D // H
G = 4
GH = H // G
E = 8
TOP_K = 2
PARTS = 3
Q_PART = [0, 0, 1, 1, 0, 2]
K_PART = [0, 1, 0, 1, 2, 0]
NB = len(Q_PART)
SHIFT_ROW = NB * HD
KROWS = SHIFT_ROW + 2
VW = 32
UNITS = G * NT
LEAD = 7
EPS = 1e-5
NEG = -1.0e38
SCALE = float(HD) ** -0.5
TWO_ONES = float(np.array([0x3F803F80], np.uint32).view(np.float32)[0])
LOCAL, FULL = 0, 1
SMAX_TILES = (2, 4)
EXPS = (1, 2)
BEHIND = [0] * NT + [2, 2, 3] * 4


def at(b, per_batch, k):
    return b * per_batch + k


def qk_bank(kind, i):
    return (i + 2) % 4 if kind == LOCAL else i


def ahead_of(kind, b, u, more):
    if u + LEAD < H:
        return [(kind, b, SMAX_TILES[kind] * (u + LEAD) + i) for i in range(SMAX_TILES[kind])]
    if kind == FULL and more:
        return [(LOCAL, b + 1, SMAX_TILES[LOCAL] * (u + LEAD - H) + i) for i in range(SMAX_TILES[LOCAL])]
    return []


def tower(nc, x, tok_w, wq, bq, wk, bk, wv, bv, wo, bo, wqkv, bqkv, wg, bg, wexp, bexp, out):
    with ExitStack() as ctx:
        def sb(name, shape, dt=F32):
            return ctx.enter_context(nc.sbuf_tensor(name, shape, dt))

        def sem(name):
            return ctx.enter_context(nc.semaphore(name))

        def both(name):
            return [sem(f"local_{name}"), sem(f"full_{name}")]

        ids = sb("ids", [P, B * NT], I32)
        h = sb("h", [P, B * NT, D])
        h2 = sb("h2", [P, NT, D])
        y = h2
        xn = [sb(f"xn{k}", [P, NT, D]) for k in (0, 1)]
        xT = [sb(f"xT{k}", [P, NC, T]) for k in (0, 1)]
        w_q = sb("w_q", [P, NC, D])
        w_k = sb("w_k", [P, NC, D])
        w_v = sb("w_v", [P, NC, D])
        w_o = sb("w_o", [P, NC, D])
        w_qkv = sb("w_qkv", [P, NC, 3 * D])
        w_gate = sb("w_gate", [P, NC, E])
        w_exp = sb("w_exp", [P, NC, E, D])
        qk_bias = [sb(f"qk_bias{k}", [P, 2, NC]) for k in (0, 1)]
        v_bias = [sb(f"v_bias{k}", [P, D]) for k in (0, 1)]
        o_bias = sb("o_bias", [P, D])
        gate_bias = sb("gate_bias", [P, E])
        exp_bias = sb("exp_bias", [E, D])
        parts = [sb(f"parts{k}", [P, 4, PARTS, T], BF16) for k in (0, 1)]
        rest = [sb(f"rest{k}", [P, 2, T]) for k in (0, 1)]
        QS = [sb(f"QS{k}", [P, H, T], BF16) for k in (0, 1)]
        KS = [sb(f"KS{k}", [P, H, T], BF16) for k in (0, 1)]
        VS = [sb(f"VS{k}", [P, NT, H, VW]) for k in (0, 1)]
        prob = sb("prob", [P, 2, GH, T])
        OT = sb("OT", [P, T])
        AO = xn[FULL]
        AOT = xT[FULL]
        AF = sb("AF", [P, NT, GH * HD])
        neg_max = [sb(f"neg_max{k}", [P, NT, H]) for k in (0, 1)]
        shift = [sb(f"shift{k}", [P, NT, 2 * GH], BF16) for k in (0, 1)]
        shiftT = [sb(f"shiftT{k}", [2 * GH, T], BF16) for k in (0, 1)]
        rden = sb("rden", [P, NT, GH])
        ident = sb("ident", [P, P])
        ident_bf = sb("ident_bf", [P, P], BF16)
        mask_q = sb("mask_q", [P, P], BF16)
        mask_k = sb("mask_k", [P, P], BF16)
        stats = sb("stats", [P, NT, 6])
        mean = [sb(f"mean{k}", [P, NT]) for k in (0, 1)]
        var = [sb(f"var{k}", [P, NT]) for k in (0, 1)]
        apart = sb("apart", [P, NT])
        rstd = [sb(f"rstd{k}", [P, NT]) for k in (0, 1)]
        var_eps = sb("var_eps", [P, NT])
        minus_half = sb("minus_half", [P, NT])
        eps = sb("eps", [P, NT])
        logit = sb("logit", [P, NT, E])
        neg_top = sb("neg_top", [P, NT])
        gexp = sb("gexp", [P, NT, E])
        gden = sb("gden", [P, NT])
        grec = sb("grec", [P, NT])
        above = prob[:, 0, 0, 0:NT * E * E].rearrange("p (t e j) -> p t e j", t=NT, e=E)
        equal = prob[:, 0, 1, 0:NT * E * E].rearrange("p (t e j) -> p t e j", t=NT, e=E)
        combT = prob[0:E, 1, 0, :]
        before = sb("before", [P, E, E])
        rank = sb("rank", [P, NT, E])
        comb = sb("comb", [P, NT, E])

        SC = [ctx.enter_context(nc.psum_tensor(f"SC{i}", [P, T], F32)) for i in (0, 1)]
        ST = ctx.enter_context(nc.psum_tensor("ST", [P, 4, T], F32))
        OB = ctx.enter_context(nc.psum_tensor("OB", [P, T], F32))
        X = ctx.enter_context(nc.psum_tensor("X", [P, T], F32))
        X_bf = X[:, :].bitcast(BF16)
        ST_local = ST[:, :, :].rearrange("p a (i w) -> p (a i) w", i=2)

        scratch = [nc.dram_tensor(f"scratch{k}", [4, P, PARTS, T], BF16).ap() for k in (0, 1)]

        s_ids = sem("ids_loaded")
        s_first = sem("first_rows_gathered")
        s_gather = sem("other_rows_gathered")
        s_w = sem("qkv_weights_loaded")
        s_w2 = sem("other_weights_loaded")
        s_const = sem("constants_set")
        s_zero = sem("zeros_set")
        s_ones = sem("ones_set")
        s_stats = both("stats")
        s_join = both("halves_joined")
        s_mv = both("meanvar")
        s_eps = both("eps_added")
        s_rstd = both("rstd")
        s_xn = both("xn")
        s_xT_ps = both("xT_in_psum")
        s_xT = both("xT")
        s_qk_ps = both("qk_in_psum")
        s_part1 = both("part1")
        s_rest = both("rest")
        s_part2 = both("part2")
        s_part3 = both("part3")
        s_v_ps = both("v_in_psum")
        s_v = both("v")
        s_written = both("parts_written")
        s_stacked = [both("stacked_low"), both("stacked_high")]
        s_sc_ps = both("row_scores")
        s_max = both("maxima")
        s_sh1 = both("shift_first_part")
        s_sh = both("shift")
        s_shT_ps = both("shift_turned")
        s_shT = both("shiftT")
        s_shrow = both("shift_rows")
        s_st_ps = both("transposed_scores")
        s_prob = both("probabilities")
        s_pv = both("unit_times_v")
        s_OT = both("OT")
        s_OT_ps = both("OT_turned")
        s_rden = both("reciprocals")
        s_norm = both("group_normalised")
        s_hb = sem("bo_added")
        s_ao_ps = sem("AO_turned")
        s_ao = sem("AOT")
        s_wo_ps = sem("projected")
        s_h2 = sem("h2")
        s_gate_ps = sem("gate_in_psum")
        s_gs = sem("gate_steps")
        s_gexp = sem("gate_exp")
        s_comb = sem("comb")
        s_comb_ps = sem("comb_turned")
        s_combT = sem("combT")
        s_eb_ps = sem("expert_bias_in_psum")
        s_y0 = sem("y_begun")
        s_moe_ps = sem("expert_in_psum")
        s_moe = sem("expert_added")
        s_yadd = sem("attention_added")
        s_out = sem("output_written")

        GATE_STEPS = 9
        QK_LOADS, OTHER_LOADS = 9, 12

        block = ctx.enter_context(nc.Block())

        @block.sync
        def _(sp):
            sp.dma_start(ids[:, :], x).then_inc(s_ids, 16)
            for dst, src in ((w_q, wq), (w_k, wk), (w_v, wv)):
                sp.dma_start(dst[:, :, :], src.rearrange("(c p) n -> p c n", p=P)).then_inc(s_w, 16)
            for j, src in enumerate((bq, bk)):
                for c in range(NC):
                    sp.dma_start(qk_bias[LOCAL][:, j, c:c + 1], src[c * P:(c + 1) * P].unsqueeze(1)).then_inc(s_w, 16)
            for dst, src in ((v_bias[LOCAL], bv), (o_bias, bo)):
                sp.dma_start(dst[:, :], src.rearrange("(a n) -> a n", a=1).to_broadcast([P, D])).then_inc(s_w, 16)
            sp.dma_start(w_o[:, :, :], wo.rearrange("(c p) n -> p c n", p=P)).then_inc(s_w2, 16)
            sp.dma_start(w_qkv[:, :, :], wqkv.rearrange("(c p) n -> p c n", p=P)).then_inc(s_w2, 16)
            sp.dma_start(w_gate[:, :, :], wg.rearrange("(c p) n -> p c n", p=P)).then_inc(s_w2, 16)
            for c in range(NC):
                sp.dma_start(w_exp[:, c, :, :], wexp[:, c * P:(c + 1) * P, :].rearrange("e p n -> p e n"))\
                    .then_inc(s_w2, 16)
            for j in range(2):
                for c in range(NC):
                    sp.dma_start(qk_bias[FULL][:, j, c:c + 1], bqkv[j * D + c * P:j * D + (c + 1) * P].unsqueeze(1))\
                        .then_inc(s_w2, 16)
            sp.dma_start(v_bias[FULL][:, :], bqkv[2 * D:3 * D].rearrange("(a n) -> a n", a=1).to_broadcast([P, D]))\
                .then_inc(s_w2, 16)
            sp.dma_start(gate_bias[:, :], bg.rearrange("(a n) -> a n", a=1).to_broadcast([P, E])).then_inc(s_w2, 16)
            sp.dma_start(exp_bias[:, :], bexp).then_inc(s_w2, 16)

            def stack(kind, b):
                for m in range(NC):
                    for i in (2 * m, 2 * m + 1):
                        sp.wait_ge(s_part3[kind], at(b, 4, i + 1))
                        sp.dma_start(scratch[kind][i], parts[kind][:, i, :, :]).then_inc(s_written[kind], 16)
                    sp.wait_ge(s_written[kind], at(b, 64, 32 * (m + 1)))
                    for j in range(NB):
                        for tile, part, dst in ((2 * m, Q_PART[j], QS), (2 * m + 1, K_PART[j], KS)):
                            src = scratch[kind][tile, :, part, :].rearrange("(n r) t -> r n t", r=HD)
                            sp.dma_start(dst[kind][j * HD:(j + 1) * HD, m * 8:(m + 1) * 8, :], src)\
                                .then_inc(s_stacked[m][kind], 16)

            def shift_rows(kind, b, g):
                sp.wait_ge(s_shT[kind], at(b, G, g + 1))
                for j in range(2):
                    sp.dma_start(QS[kind][SHIFT_ROW + j:SHIFT_ROW + j + 1, g * GH:(g + 1) * GH, :],
                                 shiftT[kind][j * GH:(j + 1) * GH, :]).then_inc(s_shrow[kind], 16)

            out_v = out.rearrange("b (w p) d -> b p w d", p=P)

            def row(b, more):
                for g in range(1, G):
                    shift_rows(LOCAL, b, g)
                if more:
                    stack(LOCAL, b + 1)
                stack(FULL, b)
                for g in range(G):
                    shift_rows(FULL, b, g)
                if more:
                    shift_rows(LOCAL, b + 1, 0)
                sp.wait_ge(s_yadd, at(b, G, G))
                sp.dma_start(out_v[b], y[:, :, :]).then_inc(s_out, 16)

            stack(LOCAL, 0)
            shift_rows(LOCAL, 0, 0)
            with sp.Fori(0, B - 1) as b:
                row(b, True)
            row(B - 1, False)
            for kind in (LOCAL, FULL):
                sp.wait_ge(s_written[kind], at(B, 64, 0))
            sp.wait_ge(s_out, at(B, 16, 1))

        @block.gpsimd
        def _(pool):
            pool.memset(minus_half[:, :], -0.5).then_inc(s_zero, 1)
            pool.memset(eps[:, :], EPS).then_inc(s_zero, 1)
            pool.memset(ident[:, :], 0.0).then_inc(s_zero, 1)
            pool.memset(ident_bf[:, :], 0.0).then_inc(s_zero, 1)
            pool.memset(mask_q[:, :], 0.0).then_inc(s_zero, 1)
            pool.memset(mask_k[:, :], 0.0).then_inc(s_zero, 1)
            pool.memset(before[:, :, :], 1.0).then_inc(s_zero, 1)

            def gather(t):
                pool.indirect_dma_start(
                    h[:, t, :], None, tok_w,
                    bass.IndirectOffsetOnAxis(ap=ids[:, t:t + 1].bitcast(U32), axis=0),
                ).then_inc(s_first if t < NT else s_gather, 16)

            pool.wait_ge(s_ids, 16)
            for t in range(NT):
                gather(t)
            pool.wait_ge(s_zero, 7)
            for m in (ident, ident_bf):
                pool.affine_select(out=m[:, :], in_=m[:, :], compare_op=ALU.not_equal, fill=1.0, base=0,
                                   pattern=[[-1, P]], channel_multiplier=1).then_inc(s_const, 1)
            pool.affine_select(out=mask_q[:, :], in_=mask_q[:, :], compare_op=ALU.is_ge, fill=NEG, base=0,
                               pattern=[[-1, P]], channel_multiplier=1).then_inc(s_const, 1)
            pool.affine_select(out=mask_k[:, :], in_=mask_k[:, :], compare_op=ALU.is_ge, fill=NEG, base=0,
                               pattern=[[1, P]], channel_multiplier=-1).then_inc(s_const, 1)
            pool.affine_select(out=before[:, :, :], in_=before[:, :, :], compare_op=ALU.is_gt, fill=0.0,
                               base=0, pattern=[[1, E], [-1, E]], channel_multiplier=0).then_inc(s_const, 1)

            def inv_std(kind, b):
                pool.wait_ge(s_mv[kind], at(b, 2, 2))
                pool.tensor_tensor(var_eps[:, :], var[kind][:, :], eps[:, :], ALU.add)\
                    .then_inc(s_eps[kind], 1)
                pool.wait_ge(s_eps[kind], at(b, 1, 1))
                pool.tensor_tensor(rstd[kind][:, :], var_eps[:, :], minus_half[:, :], ALU.pow)\
                    .then_inc(s_rstd[kind], 1)

            def third_part(kind, b, i):
                pool.wait_ge(s_part2[kind], at(b, 4, i + 1))
                pool.tensor_tensor(parts[kind][:, i, 2, :], rest[kind][:, i % 2, :], parts[kind][:, i, 1, :],
                                   ALU.subtract).then_inc(s_part3[kind], 1)

            def add_bo(b):
                pool.wait_ge(s_xn[LOCAL], at(b, NT, NT))
                for t in range(NT):
                    pool.tensor_tensor(h[:, b * NT + t, :], h[:, b * NT + t, :], o_bias[:, :], ALU.add)\
                        .then_inc(s_hb, 1)

            def row(b, more):
                if more:
                    inv_std(LOCAL, b + 1)
                    for i in range(4):
                        third_part(LOCAL, b + 1, i)
                inv_std(FULL, b)
                for i in range(4):
                    third_part(FULL, b, i)
                if more:
                    add_bo(b + 1)
                for g in range(G):
                    pool.wait_ge(s_norm[FULL], at(b, G, g + 1))
                    pool.wait_ge(s_moe, at(b, NT * E, NT * E))
                    part = y[:, :, g * GH * HD:(g + 1) * GH * HD]
                    pool.tensor_tensor(part, part, AF[:, :, :], ALU.add).then_inc(s_yadd, 1)

            inv_std(LOCAL, 0)
            for i in range(4):
                third_part(LOCAL, 0, i)
            for t in range(NT, B * NT):
                gather(t)
            pool.wait_ge(s_w, 16 * QK_LOADS)
            add_bo(0)
            with pool.Fori(0, B - 1) as b:
                row(b, True)
            row(B - 1, False)

        @block.scalar
        def _(act):
            def turn_x(kind, b):
                for c in range(NC):
                    act.wait_ge(s_xT_ps[kind], at(b, NC, c + 1))
                    act.copy(xT[kind][:, c, :], (ST[:, c, :] if kind == LOCAL else SC[c][:, :]))\
                        .then_inc(s_xT[kind], 1)

            def two_parts(kind, b, m):
                for i in (2 * m, 2 * m + 1):
                    act.wait_ge(s_qk_ps[kind], at(b, 4, i + 1))
                    act.activation(parts[kind][:, i, 0, :], ST[:, qk_bank(kind, i), :], ACT.Identity,
                                   bias=qk_bias[kind][:, i % 2, m:m + 1]).then_inc(s_part1[kind], 1)
                for i in (2 * m, 2 * m + 1):
                    act.wait_ge(s_rest[kind], at(b, 4, i + 1))
                    act.copy(parts[kind][:, i, 1, :], rest[kind][:, i % 2, :]).then_inc(s_part2[kind], 1)

            def copy_shift(kind, b, g):
                act.wait_ge(s_shT_ps[kind], at(b, G, g + 1))
                if g > 0:
                    act.wait_ge(s_shrow[kind], at(b, 32 * G, 32 * g))
                act.copy(shiftT[kind][:, :], X_bf[0:2 * GH, 0:T]).then_inc(s_shT[kind], 1)

            def copy_OT(kind, b, g):
                act.wait_ge(s_pv[kind], at(b, UNITS, NT * (g + 1)))
                if g > 0:
                    act.wait_ge(s_OT_ps[kind], at(b, G, g))
                elif kind == FULL:
                    act.wait_ge(s_OT_ps[LOCAL], at(b, G, G))
                act.copy(OT[:, :], OB[:, :]).then_inc(s_OT[kind], 1)

            def exps(kind, b, u):
                slot = u % 2
                if u >= 2:
                    act.wait_ge(s_pv[kind], at(b, UNITS, u - 1))
                elif kind == FULL:
                    act.wait_ge(s_pv[LOCAL], at(b, UNITS, UNITS))
                for e in range(EXPS[kind]):
                    n = EXPS[kind] * u + e
                    act.wait_ge(s_st_ps[kind], at(b, EXPS[kind] * UNITS, n + 1))
                    if kind == FULL:
                        dst, src = prob[:, slot, 2 * e:2 * e + 2, :], ST[:, 2 * e:2 * e + 2, :]
                    else:
                        w = 2 * P if u % NT < NT - 1 else P
                        dst, src = prob[:, slot, :, 0:w], ST_local[:, 4 * slot:4 * slot + 4, 0:w]
                    act.activation(dst, src, ACT.Exp, scale=SCALE).then_inc(s_prob[kind], 1)

            def slots(kind, b, more):
                for u in range(UNITS):
                    exps(kind, b, u)
                    if u % 4 == 1 and u < 12:
                        copy_shift(kind, b, u // 4 + 1)
                    if u == 13 and kind == FULL and more:
                        copy_shift(LOCAL, b + 1, 0)
                    if u % 4 == 0 and u > 0:
                        copy_OT(kind, b, u // 4 - 1)
                copy_OT(kind, b, G - 1)

            def row(b, more):
                slots(LOCAL, b, more)
                if more:
                    turn_x(LOCAL, b + 1)
                    two_parts(LOCAL, b + 1, 0)
                for c in range(NC):
                    act.wait_ge(s_ao_ps, at(b, NC, c + 1))
                    act.copy(AOT[:, c, :], SC[c][:, :]).then_inc(s_ao, 1)
                if more:
                    two_parts(LOCAL, b + 1, 1)
                turn_x(FULL, b)
                for m in range(NC):
                    two_parts(FULL, b, m)
                act.wait_ge(s_gs, at(b, GATE_STEPS, 3))
                act.activation(gexp[:, :, :], logit[:, :, :], ACT.Exp).then_inc(s_gexp, 1)
                act.wait_ge(s_comb_ps, at(b, 1, 1))
                act.copy(combT[:, :], X[0:E, :]).then_inc(s_combT, 1)
                copy_shift(FULL, b, 0)
                slots(FULL, b, more)

            act.wait_ge(s_w, 16 * QK_LOADS)
            turn_x(LOCAL, 0)
            for m in range(NC):
                two_parts(LOCAL, 0, m)
            copy_shift(LOCAL, 0, 0)
            act.wait_ge(s_w2, 16 * OTHER_LOADS)
            with act.Fori(0, B - 1) as b:
                row(b, True)
            row(B - 1, False)

        @block.vector
        def _(dve):
            def norm_stats(kind, b):
                for t in range(NT):
                    src = h[:, b * NT + t, :] if kind == LOCAL else h2[:, t, :]
                    dve.bn_stats(stats[:, t, :], src).then_inc(s_stats[kind], 1)
                dve.wait_ge(s_stats[kind], at(b, NT, NT))
                mean_e, sq_e, mean_o, sq_o = (stats[:, :, j] for j in (1, 2, 4, 5))
                dve.tensor_tensor(apart[:, :], mean_e, mean_o, ALU.subtract).then_inc(s_join[kind], 1)
                dve.tensor_tensor(mean[kind][:, :], mean_e, mean_o, ALU.add).then_inc(s_join[kind], 1)
                dve.tensor_tensor(var[kind][:, :], sq_e, sq_o, ALU.add).then_inc(s_join[kind], 1)
                dve.wait_ge(s_join[kind], at(b, 4, 3))
                dve.scalar_tensor_tensor(out=apart[:, :], in0=apart[:, :], scalar=0.25, in1=apart[:, :],
                                         op0=ALU.mult, op1=ALU.mult).then_inc(s_join[kind], 1)
                dve.tensor_scalar(mean[kind][:, :], mean[kind][:, :], 0.5, None, ALU.mult).then_inc(s_mv[kind], 1)
                dve.wait_ge(s_join[kind], at(b, 4, 4))
                dve.scalar_tensor_tensor(out=var[kind][:, :], in0=var[kind][:, :], scalar=1.0 / D, in1=apart[:, :],
                                         op0=ALU.mult, op1=ALU.add).then_inc(s_mv[kind], 1)

            def norm_apply(kind, b):
                dve.wait_ge(s_rstd[kind], at(b, 1, 1))
                for t in range(NT):
                    src = h[:, b * NT + t, :] if kind == LOCAL else h2[:, t, :]
                    dve.tensor_scalar(xn[kind][:, t, :], src, mean[kind][:, t:t + 1], rstd[kind][:, t:t + 1],
                                      ALU.subtract, ALU.mult).then_inc(s_xn[kind], 1)

            def leave_rest(kind, b, m):
                for i in (2 * m, 2 * m + 1):
                    dve.wait_ge(s_part1[kind], at(b, 4, i + 1))
                    if m > 0:
                        dve.wait_ge(s_part3[kind], at(b, 4, i - 1))
                    dve.scalar_tensor_tensor(out=rest[kind][:, i % 2, :], in0=ST[:, qk_bank(kind, i), :],
                                             scalar=qk_bias[kind][:, i % 2, m:m + 1],
                                             in1=parts[kind][:, i, 0, :], op0=ALU.add, op1=ALU.subtract)\
                        .then_inc(s_rest[kind], 1)

            def store_v(kind, b):
                for j in range(2):
                    dve.wait_ge(s_v_ps[kind], at(b, 2, j + 1))
                    src = ST[:, 2 + j, :] if kind == LOCAL else SC[j][:, :]
                    dve.tensor_tensor(VS[kind][:, 2 * j:2 * j + 2, :, 0:HD],
                                      src.rearrange("p (t n d) -> p t n d", t=2, n=H),
                                      v_bias[kind][:, :].rearrange("p (o n d) -> p o n d", o=1, n=H)
                                      .to_broadcast([P, 2, H, HD]), ALU.add).then_inc(s_v[kind], 1)

            def maxima(kind, b, k):
                n = SMAX_TILES[kind]
                head, i = k // n, k % n
                dve.wait_ge(s_sc_ps[kind], at(b, n * H, k + 1))
                if kind == FULL:
                    dve.tensor_reduce(neg_max[FULL][:, i, head:head + 1], SC[k % 2][:, :], AX.X, ALU.max,
                                      negate=True).then_inc(s_max[kind], 1)
                else:
                    dve.tensor_reduce(neg_max[LOCAL][:, 2 * i:2 * i + 2, head],
                                      SC[k % 2][:, :].rearrange("p (w k) -> p w k", w=2), AX.X, ALU.max,
                                      negate=True).then_inc(s_max[kind], 1)
                if (k + 1) % (n * GH) == 0:
                    g = head // GH
                    own = neg_max[kind][:, :, g * GH:(g + 1) * GH]
                    dve.wait_ge(s_max[kind], at(b, n * H, k + 1))
                    if g > 0:
                        dve.wait_ge(s_shT_ps[kind], at(b, G, g))
                    dve.tensor_copy(shift[kind][:, :, 0:GH], own).then_inc(s_sh1[kind], 1)
                    dve.wait_ge(s_sh1[kind], at(b, G, g + 1))
                    dve.tensor_tensor(shift[kind][:, :, GH:2 * GH], own, shift[kind][:, :, 0:GH], ALU.subtract)\
                        .then_inc(s_sh[kind], 1)

            def normalise(kind, b, g):
                dve.wait_ge(s_OT_ps[kind], at(b, G, g + 1))
                o = X[:, :].rearrange("p (t i v) -> p t i v", t=NT, i=GH)
                dve.reciprocal(rden[:, :, :], o[:, :, :, HD]).then_inc(s_rden[kind], 1)
                dve.wait_ge(s_rden[kind], at(b, G, g + 1))
                if kind == FULL and g > 0:
                    dve.wait_ge(s_yadd, at(b, G, g))
                dst = AF[:, :, :] if kind == FULL else AO[:, :, g * GH * HD:(g + 1) * GH * HD]
                for t in range(NT):
                    last = dve.tensor_tensor(dst[:, t, :].rearrange("p (i d) -> p i d", i=GH), o[:, t, :, 0:HD],
                                             rden[:, t, :].unsqueeze(2).to_broadcast([P, GH, HD]), ALU.mult)
                last.then_inc(s_norm[kind], 1)

            def slots(kind, b, more):
                for u in range(UNITS):
                    if u % 4 == 2 and u >= 6:
                        normalise(kind, b, u // 4 - 1)
                    for step in ahead_of(kind, b, u, more):
                        maxima(*step)
                    if kind == LOCAL and more and u == 9:
                        norm_stats(LOCAL, b + 1)
                    if kind == LOCAL and more and u == 12:
                        norm_apply(LOCAL, b + 1)
                normalise(kind, b, G - 1)

            def gate(b):
                def step(ins, k):
                    ins.then_inc(s_gs, 1)
                    dve.wait_ge(s_gs, at(b, GATE_STEPS, k))

                dve.wait_ge(s_gate_ps, at(b, 1, 1))
                step(dve.tensor_tensor(logit[:, :, :], X[:, 0:NT * E].rearrange("p (t e) -> p t e", t=NT),
                                       gate_bias[:, :].unsqueeze(1).to_broadcast([P, NT, E]), ALU.add), 1)
                step(dve.tensor_reduce(neg_top[:, :], logit[:, :, :], AX.X, ALU.max, negate=True), 2)
                step(dve.tensor_tensor(logit[:, :, :], logit[:, :, :],
                                       neg_top[:, :].unsqueeze(2).to_broadcast([P, NT, E]), ALU.add), 3)
                dve.wait_ge(s_gexp, at(b, 1, 1))
                step(dve.tensor_reduce(gden[:, :], gexp[:, :, :], AX.X, ALU.add), 4)
                dve.reciprocal(grec[:, :], gden[:, :])
                by_e = gexp[:, :, :].unsqueeze(3).to_broadcast([P, NT, E, E])
                by_j = gexp[:, :, :].unsqueeze(2).to_broadcast([P, NT, E, E])
                dve.tensor_tensor(above[:, :, :, :], by_j, by_e, ALU.is_gt)
                step(dve.tensor_tensor(equal[:, :, :, :], by_j, by_e, ALU.is_equal), 5)
                step(dve.tensor_tensor(equal[:, :, :, :], equal[:, :, :, :],
                                       before[:, :, :].unsqueeze(1).to_broadcast([P, NT, E, E]), ALU.mult), 6)
                step(dve.tensor_tensor(above[:, :, :, :], above[:, :, :, :], equal[:, :, :, :], ALU.add), 7)
                step(dve.tensor_reduce(rank[:, :, :], above[:, :, :, :], AX.X, ALU.add), 8)
                step(dve.scalar_tensor_tensor(out=rank[:, :, :], in0=rank[:, :, :], scalar=TOP_K - 0.5,
                                              in1=gexp[:, :, :], op0=ALU.is_lt, op1=ALU.mult), 9)
                dve.tensor_tensor(comb[:, :, :], rank[:, :, :],
                                  grec[:, :].unsqueeze(2).to_broadcast([P, NT, E]), ALU.mult).then_inc(s_comb, 1)

            def begin_y(b):
                for j in range(2):
                    dve.wait_ge(s_eb_ps, at(b, 2, j + 1))
                    src = (OB, X)[j][:, :].rearrange("p (t n) -> p t n", t=2)
                    dve.tensor_tensor(y[:, 2 * j:2 * j + 2, :], src, h2[:, 2 * j:2 * j + 2, :], ALU.add)\
                        .then_inc(s_y0, 1)

            def add_experts(b, s):
                t, j = s // 4, s % 4
                dve.wait_ge(s_moe_ps, at(b, NT * E // 2, s + 1))
                for e in (2 * j, 2 * j + 1):
                    if e == 0:
                        dve.wait_ge(s_y0, at(b, 2, 2))
                    else:
                        dve.wait_ge(s_moe, at(b, NT * E, t * E + e))
                    dve.scalar_tensor_tensor(out=y[:, t, :], in0=ST[:, j, (e % 2) * D:(e % 2 + 1) * D],
                                             scalar=comb[:, t, e:e + 1], in1=y[:, t, :],
                                             op0=ALU.mult, op1=ALU.add).then_inc(s_moe, 1)

            def row(b, more):
                slots(LOCAL, b, more)
                if more:
                    leave_rest(LOCAL, b + 1, 0)
                    leave_rest(LOCAL, b + 1, 1)
                dve.wait_ge(s_hb, at(b, NT, NT))
                dve.wait_ge(s_out, at(b, 16, 1))
                for j in range(2):
                    dve.wait_ge(s_wo_ps, at(b, 2, j + 1))
                    dve.tensor_tensor(h2[:, 2 * j:2 * j + 2, :],
                                      SC[j][:, :].rearrange("p (t n) -> p t n", t=2),
                                      h[:, bass.ds(b * NT + 2 * j, 2), :], ALU.add).then_inc(s_h2, 1)
                dve.wait_ge(s_h2, at(b, 2, 2))
                norm_stats(FULL, b)
                norm_apply(FULL, b)
                if more:
                    store_v(LOCAL, b + 1)
                leave_rest(FULL, b, 0)
                leave_rest(FULL, b, 1)
                store_v(FULL, b)
                gate(b)
                begin_y(b)
                k = 0
                for n, behind in enumerate(BEHIND):
                    add_experts(b, n)
                    for _ in range(behind):
                        maxima(FULL, b, k)
                        k += 1
                slots(FULL, b, more)

            def set_ones(k):
                dve.memset(KS[k][SHIFT_ROW:KROWS, :, :].bitcast(F32), TWO_ONES).then_inc(s_ones, 1)
                dve.memset(VS[k][:, :, :, HD + 1:VW], 0.0).then_inc(s_ones, 1)
                dve.memset(VS[k][:, :, :, HD:HD + 1], 1.0).then_inc(s_ones, 1)

            dve.memset(apart[:, :], 0.0).then_inc(s_out, 1)
            dve.wait_ge(s_first, 16 * NT)
            norm_stats(LOCAL, 0)
            norm_apply(LOCAL, 0)
            set_ones(LOCAL)
            dve.wait_ge(s_w, 16 * QK_LOADS)
            leave_rest(LOCAL, 0, 0)
            leave_rest(LOCAL, 0, 1)
            store_v(LOCAL, 0)
            set_ones(FULL)
            for k in range(LEAD * SMAX_TILES[LOCAL]):
                maxima(LOCAL, 0, k)
            dve.wait_ge(s_gather, 16 * NT * (B - 1))
            dve.wait_ge(s_w2, 16 * OTHER_LOADS)
            with dve.Fori(0, B - 1) as b:
                row(b, True)
            row(B - 1, False)

        @block.tensor
        def _(pe):
            def turn_x(kind, b):
                pe.wait_ge(s_xn[kind], at(b, NT, NT))
                for c in range(NC):
                    bank = ST[:, c, :] if kind == LOCAL else SC[c][:, :]
                    for t in range(NT):
                        mm = pe.transpose(bank[:, t * P:(t + 1) * P], xn[kind][:, t, c * P:(c + 1) * P], ident[:, :])
                    mm.then_inc(s_xT_ps[kind], 1)

            def project_qk(kind, b, m):
                pe.wait_ge(s_xT[kind], at(b, NC, NC))
                for j in range(2):
                    i = 2 * m + j
                    for c in range(NC):
                        w = (w_q, w_k)[j][:, c, m * P:(m + 1) * P] if kind == LOCAL else \
                            w_qkv[:, c, j * D + m * P:j * D + (m + 1) * P]
                        mm = pe.matmul(ST[:, qk_bank(kind, i), :], w, xT[kind][:, c, :],
                                       start=(c == 0), stop=(c == NC - 1))
                    mm.then_inc(s_qk_ps[kind], 1)

            def project_v(kind, b):
                for j in range(2):
                    if kind == LOCAL:
                        pe.wait_ge(s_rest[LOCAL], at(b, 4, j + 1))
                    bank = ST[:, 2 + j, :] if kind == LOCAL else SC[j][:, :]
                    for t in (2 * j, 2 * j + 1):
                        for c in range(NC):
                            w = w_v[:, c, :] if kind == LOCAL else w_qkv[:, c, 2 * D:3 * D]
                            mm = pe.matmul(bank[:, (t % 2) * D:(t % 2 + 1) * D], xT[kind][:, c, t * P:(t + 1) * P], w,
                                           start=(c == 0), stop=(c == NC - 1))
                    mm.then_inc(s_v_ps[kind], 1)

            def row_scores(kind, b, k):
                n = SMAX_TILES[kind]
                head, i = k // n, k % n
                if k >= 2:
                    pe.wait_ge(s_max[kind], at(b, n * H, k - 1))
                elif kind == FULL:
                    pe.wait_ge(s_v[FULL], at(b, 2, 2))
                elif not isinstance(b, int) or b > 0:
                    pe.wait_ge(s_max[FULL], at(b - 1, 4 * H, 4 * H))
                if head % 8 == 0 and i == 0:
                    pe.wait_ge(s_stacked[head // 8][kind], at(b, 16 * 2 * NB, 16 * 2 * NB))
                bank = SC[k % 2]
                if kind == FULL:
                    pe.matmul(bank[:, :], QS[FULL][0:SHIFT_ROW, head, i * P:(i + 1) * P], KS[FULL][0:SHIFT_ROW, head, :],
                              start=True, stop=True).then_inc(s_sc_ps[FULL], 1)
                    return
                for w in (2 * i, 2 * i + 1):
                    q = QS[LOCAL][0:SHIFT_ROW, head, w * P:(w + 1) * P]
                    o = (w % 2) * 2 * P
                    if w > 0:
                        pe.matmul(bank[:, o:o + 2 * P], q, KS[LOCAL][0:SHIFT_ROW, head, (w - 1) * P:(w + 1) * P],
                                  start=(w % 2 == 0), stop=False, skip_group_check=True)
                    else:
                        for j in range(2):
                            pe.matmul(bank[:, j * P:(j + 1) * P], q, KS[LOCAL][0:SHIFT_ROW, head, 0:P],
                                      start=(j == 0), stop=False, skip_group_check=True)
                        pe.matmul(bank[:, 0:P], ident_bf[:, :], mask_q[:, :], start=False, stop=False,
                                  skip_group_check=True)
                    mm = pe.matmul(bank[:, o + P:o + 2 * P], ident_bf[:, :], mask_q[:, :], start=False,
                                   stop=(w % 2 == 1), skip_group_check=True)
                mm.then_inc(s_sc_ps[LOCAL], 1)

            def turn_shift(kind, b, g):
                pe.wait_ge(s_sh[kind], at(b, G, g + 1))
                for t in range(NT):
                    mm = pe.transpose(X_bf[0:2 * GH, t * P:(t + 1) * P], shift[kind][:, t, :], ident_bf[:, :])
                mm.then_inc(s_shT_ps[kind], 1)

            def scores(kind, b, u, e):
                g, kt = u // NT, u % NT
                if kt == 0 and e == 0:
                    pe.wait_ge(s_shrow[kind], at(b, 32 * G, 32 * (g + 1)))
                keys = slice(kt * P, (kt + 1) * P)
                if kind == FULL:
                    if u > 0:
                        pe.wait_ge(s_prob[FULL], at(b, 2 * UNITS, 2 * (u - 1) + e + 1))
                    else:
                        pe.wait_ge(s_moe, at(b, NT * E, NT * E))
                    for i in (2 * e, 2 * e + 1):
                        head = g * GH + i
                        mm = pe.matmul(ST[:, i, :], KS[FULL][0:KROWS, head, keys], QS[FULL][0:KROWS, head, :],
                                       start=True, stop=True)
                    mm.then_inc(s_st_ps[FULL], 1)
                    return
                if u >= 2:
                    pe.wait_ge(s_prob[LOCAL], at(b, UNITS, u - 1))
                w = 2 * P if kt < NT - 1 else P
                for i in range(GH):
                    head = g * GH + i
                    bank = ST_local[:, 4 * (u % 2) + i, :]
                    pe.matmul(bank[:, 0:w], KS[LOCAL][0:KROWS, head, keys], QS[LOCAL][0:KROWS, head, kt * P:kt * P + w],
                              start=(i % 2 == 0), stop=False, skip_group_check=True)
                    mm = pe.matmul(bank[:, 0:P], ident_bf[:, :], mask_k[:, :], start=False, stop=(i % 2 == 1),
                                   skip_group_check=True)
                mm.then_inc(s_st_ps[LOCAL], 1)

            def times_v(kind, b, u, half=0):
                g, kt = u // NT, u % NT
                pe.wait_ge(s_prob[kind], at(b, EXPS[kind] * UNITS, EXPS[kind] * (u + 1)))
                if u == 0:
                    pe.wait_ge(s_v[kind], at(b, 2, 2))
                if kt == 0:
                    if g > 0:
                        pe.wait_ge(s_OT[kind], at(b, G, g))
                    elif kind == FULL:
                        pe.wait_ge(s_y0, at(b, 2, 1))
                w = 2 * P if kt < NT - 1 else P
                columns = slice(half * 2 * P, (half + 1) * 2 * P) if kind == FULL else slice(kt * P, kt * P + w)
                source = columns if kind == FULL else slice(0, w)
                for i in range(GH):
                    mm = pe.matmul(OB[VW * i:VW * (i + 1), columns], VS[kind][:, kt, g * GH + i, :],
                                   prob[:, u % 2, i, source], start=(kt == 0 and half == 0),
                                   stop=(kt == NT - 1), skip_group_check=True)
                if kind == LOCAL or half == 1:
                    mm.then_inc(s_pv[kind], 1)

            def turn_O(kind, b, g):
                pe.wait_ge(s_OT[kind], at(b, G, g + 1))
                for t in range(NT):
                    mm = pe.transpose(X[:, t * P:(t + 1) * P], OT[:, t * P:(t + 1) * P], ident[:, :])
                mm.then_inc(s_OT_ps[kind], 1)

            def slots(kind, b, more):
                for u in range(UNITS):
                    ahead = ahead_of(kind, b, u, more)
                    quarters = [ahead[i * len(ahead) // 4:(i + 1) * len(ahead) // 4] for i in range(4)]
                    scores(kind, b, u, 0)
                    if kind == FULL:
                        for step in quarters[0]:
                            row_scores(*step)
                        scores(kind, b, u, 1)
                        for step in quarters[1]:
                            row_scores(*step)
                    else:
                        for step in quarters[0] + quarters[1]:
                            row_scores(*step)
                    if u % 4 == 1 and u < 12:
                        pe.wait_ge(s_shT[kind], at(b, G, u // 4 + 1))
                        if u == 9:
                            pe.wait_ge(s_norm[kind], at(b, G, 1))
                        turn_shift(kind, b, u // 4 + 1)
                    if u == 13 and kind == FULL and more:
                        pe.wait_ge(s_norm[FULL], at(b, G, 2))
                        turn_shift(LOCAL, b + 1, 0)
                    if u > 0:
                        times_v(kind, b, u - 1)
                    for step in quarters[2]:
                        row_scores(*step)
                    if u > 0 and kind == FULL:
                        times_v(kind, b, u - 1, 1)
                    for step in quarters[3]:
                        row_scores(*step)
                    if u % 4 == 1 and u >= 5:
                        if u < 12:
                            pe.wait_ge(s_shT[kind], at(b, G, u // 4 + 2))
                        else:
                            pe.wait_ge(s_norm[kind], at(b, G, 2))
                        if u == 13 and kind == FULL and more:
                            pe.wait_ge(s_shT[LOCAL], at(b + 1, G, 1))
                        turn_O(kind, b, u // 4 - 1)
                for half in range(1 + kind):
                    times_v(kind, b, UNITS - 1, half)

            def last_group(kind, b):
                pe.wait_ge(s_norm[kind], at(b, G, G - 1))
                turn_O(kind, b, G - 1)

            def two_experts(b, s):
                t, j = s // 4, s % 4
                if t == 0:
                    pe.wait_ge(s_rest[FULL], at(b, 4, j + 1))
                else:
                    pe.wait_ge(s_moe, at(b, NT * E, (t - 1) * E + 2 * j + 2))
                for c in range(NC):
                    mm = pe.matmul(ST[:, j, :], xT[FULL][:, c, t * P:(t + 1) * P], w_exp[:, c, 2 * j:2 * j + 2, :],
                                   start=(c == 0), stop=(c == NC - 1))
                mm.then_inc(s_moe_ps, 1)

            def row(b, more):
                slots(LOCAL, b, more)
                if more:
                    turn_x(LOCAL, b + 1)
                last_group(LOCAL, b)
                if more:
                    project_qk(LOCAL, b + 1, 0)
                pe.wait_ge(s_norm[LOCAL], at(b, G, G))
                for c in range(NC):
                    for t in range(NT):
                        mm = pe.transpose(SC[c][:, t * P:(t + 1) * P], AO[:, t, c * P:(c + 1) * P], ident[:, :])
                    mm.then_inc(s_ao_ps, 1)
                if more:
                    project_qk(LOCAL, b + 1, 1)
                pe.wait_ge(s_ao, at(b, NC, NC))
                for j in range(2):
                    for t in (2 * j, 2 * j + 1):
                        for c in range(NC):
                            mm = pe.matmul(SC[j][:, (t % 2) * D:(t % 2 + 1) * D], AOT[:, c, t * P:(t + 1) * P],
                                           w_o[:, c, :], start=(c == 0), stop=(c == NC - 1))
                    mm.then_inc(s_wo_ps, 1)
                if more:
                    project_v(LOCAL, b + 1)
                turn_x(FULL, b)
                if more:
                    pe.wait_ge(s_rest[LOCAL], at(b + 1, 4, 4))
                    pe.wait_ge(s_v[LOCAL], at(b + 1, 2, 2))
                for m in range(NC):
                    project_qk(FULL, b, m)
                project_v(FULL, b)
                for t in range(NT):
                    for c in range(NC):
                        mm = pe.matmul(X[:, t * E:(t + 1) * E], xT[FULL][:, c, t * P:(t + 1) * P], w_gate[:, c, :],
                                       start=(c == 0), stop=(c == NC - 1))
                mm.then_inc(s_gate_ps, 1)
                for n in range(4):
                    two_experts(b, n)
                pe.wait_ge(s_comb, at(b, 1, 1))
                for t in range(NT):
                    mm = pe.transpose(X[0:E, t * P:(t + 1) * P], comb[:, t, :], ident[:, :])
                mm.then_inc(s_comb_ps, 1)
                pe.wait_ge(s_combT, at(b, 1, 1))
                for j in range(2):
                    for t in (2 * j, 2 * j + 1):
                        mm = pe.matmul((OB, X)[j][:, (t % 2) * D:(t % 2 + 1) * D], combT[:, t * P:(t + 1) * P],
                                       exp_bias[:, :], start=True, stop=True)
                    mm.then_inc(s_eb_ps, 1)
                k = 0
                for n in range(4, 4 * NT):
                    two_experts(b, n)
                    for _ in range(BEHIND[n]):
                        row_scores(FULL, b, k)
                        k += 1
                pe.wait_ge(s_y0, at(b, 2, 2))
                turn_shift(FULL, b, 0)
                slots(FULL, b, more)
                last_group(FULL, b)

            pe.wait_ge(s_const, 5)
            pe.wait_ge(s_w, 16 * QK_LOADS)
            turn_x(LOCAL, 0)
            project_qk(LOCAL, 0, 0)
            project_qk(LOCAL, 0, 1)
            project_v(LOCAL, 0)
            for k in range(LEAD * SMAX_TILES[LOCAL]):
                row_scores(LOCAL, 0, k)
            turn_shift(LOCAL, 0, 0)
            pe.wait_ge(s_rest[LOCAL], 4)
            pe.wait_ge(s_v[LOCAL], 2)
            pe.wait_ge(s_ones, 6)
            pe.wait_ge(s_w2, 16 * OTHER_LOADS)
            with pe.Fori(0, B - 1) as b:
                row(b, True)
            row(B - 1, False)


_INS = ['x', 'L0_tok_W', 'L0_attn_Wq', 'L0_attn_bq', 'L0_attn_Wk', 'L0_attn_bk', 'L0_attn_Wv', 'L0_attn_bv',
        'L0_attn_Wo', 'L0_attn_bo', 'L0_ffn_W_qkv', 'L0_ffn_b_qkv', 'L0_ffn_W_gate', 'L0_ffn_b_gate',
        'L0_ffn_W_experts', 'L0_ffn_b_experts']


def kernel(**inputs):
    import concourse.bacc as bacc
    from concourse.bass_utils import run_bass_kernel_spmd

    nc = bacc.Bacc("TRN2", target_bir_lowering=False, num_devices=1)
    arrays, args = {}, []
    for name in _INS:
        a = np.asarray(inputs[name])
        if name == 'x':
            a = a.reshape(B * NT, P).T
        a = np.ascontiguousarray(a)
        arrays[f"in_{name}"] = a
        args.append(nc.dram_tensor(f"in_{name}", a.shape, mybir.dt.from_np(a.dtype), kind="ExternalInput").ap())
    out = nc.dram_tensor("out", (B, T, D), F32, kind="ExternalOutput").ap()
    tower(nc, *args, out)
    result = run_bass_kernel_spmd(nc, [arrays], core_ids=[0])
    return result.results[0]["out"]
```

```python
from contextlib import ExitStack

import numpy as np

import concourse.bass as bass
from concourse import mybir

F32 = mybir.dt.float32
BF16 = mybir.dt.bfloat16
I32 = mybir.dt.int32
U32 = mybir.dt.uint32
ALU = mybir.AluOpType
ACT = mybir.ActivationFunctionType
AX = mybir.AxisListType

P = 128
B = 4
T = 512
NT = T // P
D = 256
NC = D // P
H = 16
HD = D // H
G = 4
GH = H // G
E = 8
TOP_K = 2
PARTS = 3
K_OF_Q = (3, 2, 1)
NB = sum(K_OF_Q)
SHIFT_ROW = NB * HD
KROWS = SHIFT_ROW + 2
VW = 32
UNITS = G * NT
LEAD = (7, 6)
EPS = 1e-5
NEG = -1.0e38
SCALE = float(HD) ** -0.5
TWO_ONES = float(np.array([0x3F803F80], np.uint32).view(np.float32)[0])
LOCAL, FULL = 0, 1
SMAX_TILES = (2, 4)
EXPS = (1, 2)
PAIRS = NT * E // 4
BESIDE = [0, 0, 4, 4, 4, 4, 4, 4, 0]
BIAS_PAIR = 2
WARM = (11, 16, 15)
FIRST_SHIFT = 2


def at(b, per_batch, k):
    return b * per_batch + k


def expert_bank(s):
    return 2 * (s // E) + s % 2, s % E // 2, s % 4


def ahead_of(kind, b, u, more):
    head = u + LEAD[kind]
    if head < H:
        return [(kind, b, SMAX_TILES[kind] * head + i) for i in range(SMAX_TILES[kind])]
    if kind == FULL and more:
        first, end = (-(-SMAX_TILES[LOCAL] * LEAD[LOCAL] * (head - H + j) // LEAD[FULL]) for j in (0, 1))
        return [(LOCAL, b + 1, k) for k in range(first, end)]
    return []


def tower(nc, x, tok_w, wq, bq, wk, bk, wv, bv, wo, bo, wqkv, bqkv, wg, bg, wexp, bexp, out):
    with ExitStack() as ctx:
        def sb(name, shape, dt=F32):
            return ctx.enter_context(nc.sbuf_tensor(name, shape, dt))

        def sem(name):
            return ctx.enter_context(nc.semaphore(name))

        def both(name):
            return [sem(f"local_{name}"), sem(f"full_{name}")]

        ids = sb("ids", [P, B * NT], I32)
        h = sb("h", [P, B * NT, D])
        h2 = sb("h2", [P, NT, D])
        y = h2
        xn = [sb(f"xn{k}", [P, NT, D]) for k in (0, 1)]
        xT = [sb(f"xT{k}", [P, NC, T]) for k in (0, 1)]
        w_q = sb("w_q", [P, NC, D])
        w_k = sb("w_k", [P, NC, D])
        w_v = sb("w_v", [P, NC, D])
        w_o = sb("w_o", [P, NC, D])
        w_qkv = sb("w_qkv", [P, NC, 3 * D])
        w_gate = sb("w_gate", [P, NC, E])
        w_exp = sb("w_exp", [P, NC, E, D])
        qk_bias = [sb(f"qk_bias{k}", [P, 2, NC]) for k in (0, 1)]
        v_bias = [sb(f"v_bias{k}", [P, D]) for k in (0, 1)]
        o_bias = sb("o_bias", [P, D])
        gate_bias = sb("gate_bias", [P, E])
        exp_bias = sb("exp_bias", [E, D])
        parts = [sb(f"parts{k}", [P, 4, PARTS, T], BF16) for k in (0, 1)]
        rest = [sb(f"rest{k}", [P, 2, T]) for k in (0, 1)]
        QS = [sb(f"QS{k}", [P, H, T], BF16) for k in (0, 1)]
        KS = [sb(f"KS{k}", [P, H, T], BF16) for k in (0, 1)]
        VS = [sb(f"VS{k}", [P, NT, H, VW]) for k in (0, 1)]
        prob = sb("prob", [P, 2, GH, T])
        OT = sb("OT", [P, T])
        AO = xn[FULL]
        AOT = xT[FULL]
        AF = sb("AF", [P, NT, GH * HD])
        neg_max = [sb(f"neg_max{k}", [P, NT, H]) for k in (0, 1)]
        shift = [sb(f"shift{k}", [P, NT, 2 * GH], BF16) for k in (0, 1)]
        shiftT = [sb(f"shiftT{k}", [2 * GH, T], BF16) for k in (0, 1)]
        rden = sb("rden", [P, NT, GH])
        ident = sb("ident", [P, P])
        ident_bf = sb("ident_bf", [P, P], BF16)
        mask_q = sb("mask_q", [P, P], BF16)
        mask_k = sb("mask_k", [P, P], BF16)
        stats = sb("stats", [P, NT, 6])
        mean = [sb(f"mean{k}", [P, NT]) for k in (0, 1)]
        var = [sb(f"var{k}", [P, NT]) for k in (0, 1)]
        apart = sb("apart", [P, NT])
        rstd = [sb(f"rstd{k}", [P, NT]) for k in (0, 1)]
        var_eps = sb("var_eps", [P, NT])
        minus_half = sb("minus_half", [P, NT])
        eps = sb("eps", [P, NT])
        logit = sb("logit", [P, NT, E])
        neg_top = sb("neg_top", [P, NT])
        gexp = sb("gexp", [P, NT, E])
        gden = sb("gden", [P, NT])
        grec = sb("grec", [P, NT])
        above = prob[:, 0, 0, 0:NT * E * E].rearrange("p (t e j) -> p t e j", t=NT, e=E)
        equal = prob[:, 0, 1, 0:NT * E * E].rearrange("p (t e j) -> p t e j", t=NT, e=E)
        combT = prob[0:E, 1, 0, :]
        before = sb("before", [P, E, E])
        rank = sb("rank", [P, NT, E])
        comb = sb("comb", [P, NT, E])

        SC = [ctx.enter_context(nc.psum_tensor(f"SC{i}", [P, T], F32)) for i in (0, 1)]
        ST = ctx.enter_context(nc.psum_tensor("ST", [P, 4, T], F32))
        OB = ctx.enter_context(nc.psum_tensor("OB", [P, T], F32))
        X = ctx.enter_context(nc.psum_tensor("X", [P, T], F32))
        X_bf = X[:, :].bitcast(BF16)
        ST_local = ST[:, :, :].rearrange("p a (i w) -> p (a i) w", i=2)
        xT_bank = [[SC[0][:, :], SC[1][:, :]], [ST[:, 0, :], ST[:, 1, :]]]
        qk_bank = [[SC[0][:, :], SC[1][:, :], ST[:, 2, :], ST[:, 3, :]], [ST[:, i, :] for i in (2, 3, 0, 1)]]
        v_bank = [[SC[0], SC[1]], [SC[0], X]]

        scratch = [nc.dram_tensor(f"scratch{k}", [4, HD, PARTS, 8, T], BF16).ap() for k in (0, 1)]

        s_ids = sem("ids_loaded")
        s_first = sem("first_rows_gathered")
        s_gather = sem("other_rows_gathered")
        s_w = sem("qkv_weights_loaded")
        s_w2 = sem("other_weights_loaded")
        s_const = sem("constants_set")
        s_zero = sem("zeros_set")
        s_ones = sem("ones_set")
        s_stats = both("stats")
        s_join = both("halves_joined")
        s_mv = both("meanvar")
        s_eps = both("eps_added")
        s_rstd = both("rstd")
        s_xn = both("xn")
        s_xT_ps = both("xT_in_psum")
        s_xT = both("xT")
        s_qk_ps = both("qk_in_psum")
        s_part1 = both("part1")
        s_rest = both("rest")
        s_part2 = both("part2")
        s_part3 = both("part3")
        s_v_ps = both("v_in_psum")
        s_v = both("v")
        s_written = both("parts_written")
        s_stacked = [both("stacked_low"), both("stacked_high")]
        s_sc_ps = both("row_scores")
        s_max = both("maxima")
        s_sh1 = both("shift_first_part")
        s_sh = both("shift")
        s_shT_ps = both("shift_turned")
        s_shT = both("shiftT")
        s_shrow = both("shift_rows")
        s_st_ps = both("transposed_scores")
        s_prob = both("probabilities")
        s_pv = both("unit_times_v")
        s_OT = both("OT")
        s_OT_ps = both("OT_turned")
        s_rden = both("reciprocals")
        s_norm = both("group_normalised")
        s_hb = sem("bo_added")
        s_ao_ps = sem("AO_turned")
        s_ao = sem("AOT")
        s_wo_ps = sem("projected")
        s_h2 = sem("h2")
        s_gate_ps = sem("gate_in_psum")
        s_gs = sem("gate_steps")
        s_gexp = sem("gate_exp")
        s_comb = sem("comb")
        s_comb_ps = sem("comb_turned")
        s_combT = sem("combT")
        s_eb_ps = sem("expert_bias_in_psum")
        s_yb = sem("biases_added")
        s_moe_ps = sem("expert_in_psum")
        s_moe = sem("expert_added")
        s_yadd = sem("attention_added")
        s_out = sem("output_written")

        GATE_STEPS = 9
        QK_LOADS, OTHER_LOADS = 9, 12
        STACK_LOADS = 16 * 2 * PARTS

        block = ctx.enter_context(nc.Block())

        @block.sync
        def _(sp):
            sp.dma_start(ids[:, :], x).then_inc(s_ids, 16)
            for dst, src in ((w_q, wq), (w_k, wk), (w_v, wv)):
                sp.dma_start(dst[:, :, :], src.rearrange("(c p) n -> p c n", p=P)).then_inc(s_w, 16)
            for j, src in enumerate((bq, bk)):
                for c in range(NC):
                    sp.dma_start(qk_bias[LOCAL][:, j, c:c + 1], src[c * P:(c + 1) * P].unsqueeze(1)).then_inc(s_w, 16)
            for dst, src in ((v_bias[LOCAL], bv), (o_bias, bo)):
                sp.dma_start(dst[:, :], src.rearrange("(a n) -> a n", a=1).to_broadcast([P, D])).then_inc(s_w, 16)
            sp.dma_start(w_o[:, :, :], wo.rearrange("(c p) n -> p c n", p=P)).then_inc(s_w2, 16)
            sp.dma_start(w_qkv[:, :, :], wqkv.rearrange("(c p) n -> p c n", p=P)).then_inc(s_w2, 16)
            sp.dma_start(w_gate[:, :, :], wg.rearrange("(c p) n -> p c n", p=P)).then_inc(s_w2, 16)
            for c in range(NC):
                sp.dma_start(w_exp[:, c, :, :], wexp[:, c * P:(c + 1) * P, :].rearrange("e p n -> p e n"))\
                    .then_inc(s_w2, 16)
            for j in range(2):
                for c in range(NC):
                    sp.dma_start(qk_bias[FULL][:, j, c:c + 1], bqkv[j * D + c * P:j * D + (c + 1) * P].unsqueeze(1))\
                        .then_inc(s_w2, 16)
            sp.dma_start(v_bias[FULL][:, :], bqkv[2 * D:3 * D].rearrange("(a n) -> a n", a=1).to_broadcast([P, D]))\
                .then_inc(s_w2, 16)
            sp.dma_start(gate_bias[:, :], bg.rearrange("(a n) -> a n", a=1).to_broadcast([P, E])).then_inc(s_w2, 16)
            sp.dma_start(exp_bias[:, :], bexp).then_inc(s_w2, 16)

            def stack(kind, b, m):
                for i in (2 * m, 2 * m + 1):
                    for a, s_part in enumerate((s_part1, s_part2, s_part3)):
                        sp.wait_ge(s_part[kind], at(b, 4, i + 1))
                        sp.dma_start(scratch[kind][i, :, a].rearrange("r n t -> n r t"), parts[kind][:, i, a, :])\
                            .then_inc(s_written[kind], 16)
                sp.wait_ge(s_written[kind], at(b, 64 * PARTS, 32 * PARTS * (m + 1)))
                heads, at_row = slice(8 * m, 8 * (m + 1)), 0
                for a, n in enumerate(K_OF_Q):
                    rows = slice(at_row, at_row + n * HD)
                    at_row += n * HD
                    q, k = (scratch[kind][2 * m + j].rearrange("r a n t -> r a (n t)") for j in (0, 1))
                    for dst, src in ((QS, q[:, a:a + 1].to_broadcast([HD, n, 8 * T])), (KS, k[:, 0:n])):
                        sp.dma_start(dst[kind][rows, heads, :].rearrange("r n t -> r (n t)"), src)\
                            .then_inc(s_stacked[m][kind], 16)

            def shift_rows(kind, b, g):
                sp.wait_ge(s_shT[kind], at(b, G, g + 1))
                for j in range(2):
                    sp.dma_start(QS[kind][SHIFT_ROW + j:SHIFT_ROW + j + 1, g * GH:(g + 1) * GH, :],
                                 shiftT[kind][j * GH:(j + 1) * GH, :]).then_inc(s_shrow[kind], 16)

            out_v = out.rearrange("b (w p) d -> b p w d", p=P)

            def row(b, more):
                for g in range(1, G):
                    shift_rows(LOCAL, b, g)
                if more:
                    stack(LOCAL, b + 1, 0)
                for m in range(NC):
                    stack(FULL, b, m)
                if more:
                    stack(LOCAL, b + 1, 1)
                for g in range(G):
                    shift_rows(FULL, b, g)
                if more:
                    shift_rows(LOCAL, b + 1, 0)
                sp.wait_ge(s_yadd, at(b, G, G))
                sp.dma_start(out_v[b], y[:, :, :]).then_inc(s_out, 16)

            for m in range(NC):
                stack(LOCAL, 0, m)
            shift_rows(LOCAL, 0, 0)
            with sp.Fori(0, B - 1) as b:
                row(b, True)
            row(B - 1, False)
            for kind in (LOCAL, FULL):
                sp.wait_ge(s_written[kind], at(B, 64 * PARTS, 0))
            sp.wait_ge(s_out, at(B, 16, 1))

        @block.gpsimd
        def _(pool):
            pool.memset(minus_half[:, :], -0.5).then_inc(s_zero, 1)
            pool.memset(eps[:, :], EPS).then_inc(s_zero, 1)
            pool.memset(ident[:, :], 0.0).then_inc(s_zero, 1)
            pool.memset(ident_bf[:, :], 0.0).then_inc(s_zero, 1)
            pool.memset(mask_q[:, :], 0.0).then_inc(s_zero, 1)
            pool.memset(mask_k[:, :], 0.0).then_inc(s_zero, 1)
            pool.memset(before[:, :, :], 1.0).then_inc(s_zero, 1)

            def gather(t):
                pool.indirect_dma_start(
                    h[:, t, :], None, tok_w,
                    bass.IndirectOffsetOnAxis(ap=ids[:, t:t + 1].bitcast(U32), axis=0),
                ).then_inc(s_first if t < NT else s_gather, 16)

            pool.wait_ge(s_ids, 16)
            for t in range(NT):
                gather(t)
            pool.wait_ge(s_zero, 7)
            for m in (ident, ident_bf):
                pool.affine_select(out=m[:, :], in_=m[:, :], compare_op=ALU.not_equal, fill=1.0, base=0,
                                   pattern=[[-1, P]], channel_multiplier=1).then_inc(s_const, 1)
            pool.affine_select(out=mask_q[:, :], in_=mask_q[:, :], compare_op=ALU.is_ge, fill=NEG, base=0,
                               pattern=[[-1, P]], channel_multiplier=1).then_inc(s_const, 1)
            pool.affine_select(out=mask_k[:, :], in_=mask_k[:, :], compare_op=ALU.is_ge, fill=NEG, base=0,
                               pattern=[[1, P]], channel_multiplier=-1).then_inc(s_const, 1)
            pool.affine_select(out=before[:, :, :], in_=before[:, :, :], compare_op=ALU.is_gt, fill=0.0,
                               base=0, pattern=[[1, E], [-1, E]], channel_multiplier=0).then_inc(s_const, 1)

            def inv_std(kind, b):
                pool.wait_ge(s_mv[kind], at(b, 2, 2))
                pool.tensor_tensor(var_eps[:, :], var[kind][:, :], eps[:, :], ALU.add)\
                    .then_inc(s_eps[kind], 1)
                pool.wait_ge(s_eps[kind], at(b, 1, 1))
                pool.tensor_tensor(rstd[kind][:, :], var_eps[:, :], minus_half[:, :], ALU.pow)\
                    .then_inc(s_rstd[kind], 1)

            def third_part(kind, b, i):
                pool.wait_ge(s_part2[kind], at(b, 4, i + 1))
                pool.tensor_tensor(parts[kind][:, i, 2, :], rest[kind][:, i % 2, :], parts[kind][:, i, 1, :],
                                   ALU.subtract).then_inc(s_part3[kind], 1)

            def add_bo(b):
                pool.wait_ge(s_xn[LOCAL], at(b, NT, NT))
                for t in range(NT):
                    pool.tensor_tensor(h[:, b * NT + t, :], h[:, b * NT + t, :], o_bias[:, :], ALU.add)\
                        .then_inc(s_hb, 1)

            def row(b, more):
                if more:
                    inv_std(LOCAL, b + 1)
                    for i in (0, 1):
                        third_part(LOCAL, b + 1, i)
                inv_std(FULL, b)
                if more:
                    for i in (2, 3):
                        third_part(LOCAL, b + 1, i)
                for i in range(4):
                    third_part(FULL, b, i)
                if more:
                    add_bo(b + 1)
                for g in range(G):
                    pool.wait_ge(s_norm[FULL], at(b, G, g + 1))
                    pool.wait_ge(s_moe, at(b, NT * E, NT * E))
                    part = y[:, :, g * GH * HD:(g + 1) * GH * HD]
                    pool.tensor_tensor(part, part, AF[:, :, :], ALU.add).then_inc(s_yadd, 1)

            inv_std(LOCAL, 0)
            for i in range(4):
                third_part(LOCAL, 0, i)
            pool.wait_ge(s_w, 16 * QK_LOADS)
            add_bo(0)
            pool.wait_ge(s_stacked[1][LOCAL], STACK_LOADS)
            for t in range(NT, B * NT):
                gather(t)
            with pool.Fori(0, B - 1) as b:
                row(b, True)
            row(B - 1, False)

        @block.scalar
        def _(act):
            def first_part(kind, b, i):
                act.wait_ge(s_qk_ps[kind], at(b, 4, i + 1))
                act.activation(parts[kind][:, i, 0, :], qk_bank[kind][i], ACT.Identity,
                               bias=qk_bias[kind][:, i % 2, i // 2:i // 2 + 1]).then_inc(s_part1[kind], 1)

            def second_part(kind, b, i):
                act.wait_ge(s_rest[kind], at(b, 4, i + 1))
                act.copy(parts[kind][:, i, 1, :], rest[kind][:, i % 2, :]).then_inc(s_part2[kind], 1)

            def copy_AO(b, c):
                act.wait_ge(s_ao_ps, at(b, NC, c + 1))
                act.copy(AOT[:, c, :], ST[:, c, :]).then_inc(s_ao, 1)

            def copy_shift(kind, b, g):
                act.wait_ge(s_shT_ps[kind], at(b, G, g + 1))
                if g > 0:
                    act.wait_ge(s_shrow[kind], at(b, 32 * G, 32 * g))
                act.copy(shiftT[kind][:, :], X_bf[0:2 * GH, 0:T]).then_inc(s_shT[kind], 1)

            def copy_OT(kind, b, g):
                act.wait_ge(s_pv[kind], at(b, UNITS, NT * (g + 1)))
                if g > 0:
                    act.wait_ge(s_OT_ps[kind], at(b, G, g))
                elif kind == FULL:
                    act.wait_ge(s_OT_ps[LOCAL], at(b, G, G))
                act.copy(OT[:, :], OB[:, :]).then_inc(s_OT[kind], 1)

            def exps(kind, b, u):
                slot = u % 2
                if u >= 2:
                    act.wait_ge(s_pv[kind], at(b, UNITS, u - 1))
                elif kind == FULL:
                    act.wait_ge(s_pv[LOCAL], at(b, UNITS, UNITS))
                for e in range(EXPS[kind]):
                    n = EXPS[kind] * u + e
                    act.wait_ge(s_st_ps[kind], at(b, EXPS[kind] * UNITS, n + 1))
                    if kind == FULL:
                        dst, src = prob[:, slot, 2 * e:2 * e + 2, :], ST[:, 2 * e:2 * e + 2, :]
                    else:
                        w = 2 * P if u % NT < NT - 1 else P
                        dst, src = prob[:, slot, :, 0:w], ST_local[:, 4 * slot:4 * slot + 4, 0:w]
                    act.activation(dst, src, ACT.Exp, scale=SCALE).then_inc(s_prob[kind], 1)

            def slots(kind, b, more):
                for u in range(UNITS):
                    exps(kind, b, u)
                    if u % 4 == 1 + kind and u < 12:
                        copy_shift(kind, b, u // 4 + 1)
                    if u == 14 and kind == FULL and more:
                        copy_shift(LOCAL, b + 1, 0)
                    if u % 4 == 0 and u > 0:
                        copy_OT(kind, b, u // 4 - 1)
                copy_OT(kind, b, G - 1)

            def row(b, more):
                slots(LOCAL, b, more)
                copy_AO(b, 0)
                if more:
                    first_part(LOCAL, b + 1, 0)
                    first_part(LOCAL, b + 1, 1)
                copy_AO(b, 1)
                if more:
                    second_part(LOCAL, b + 1, 0)
                    second_part(LOCAL, b + 1, 1)
                    first_part(LOCAL, b + 1, 2)
                    first_part(LOCAL, b + 1, 3)
                for c in range(NC):
                    act.wait_ge(s_xT_ps[FULL], at(b, NC, c + 1))
                    act.copy(xT[FULL][:, c, :], xT_bank[FULL][c]).then_inc(s_xT[FULL], 1)
                if more:
                    second_part(LOCAL, b + 1, 2)
                    second_part(LOCAL, b + 1, 3)
                act.wait_ge(s_gs, at(b, GATE_STEPS, 3))
                act.activation(gexp[:, :, :], logit[:, :, :], ACT.Exp).then_inc(s_gexp, 1)
                for m in range(NC):
                    first_part(FULL, b, 2 * m)
                    first_part(FULL, b, 2 * m + 1)
                    second_part(FULL, b, 2 * m)
                    second_part(FULL, b, 2 * m + 1)
                act.wait_ge(s_comb_ps, at(b, 1, 1))
                act.copy(combT[:, :], X[0:E, :]).then_inc(s_combT, 1)
                copy_shift(FULL, b, 0)
                slots(FULL, b, more)

            act.wait_ge(s_w, 16 * QK_LOADS)
            for m in range(NC):
                first_part(LOCAL, 0, 2 * m)
                first_part(LOCAL, 0, 2 * m + 1)
                second_part(LOCAL, 0, 2 * m)
                second_part(LOCAL, 0, 2 * m + 1)
            copy_shift(LOCAL, 0, 0)
            act.wait_ge(s_w2, 16 * OTHER_LOADS)
            with act.Fori(0, B - 1) as b:
                row(b, True)
            row(B - 1, False)

        @block.vector
        def _(dve):
            def row_stats(kind, b, t):
                src = h[:, b * NT + t, :] if kind == LOCAL else h2[:, t, :]
                dve.bn_stats(stats[:, t, :], src).then_inc(s_stats[kind], 1)

            def mean_var(kind, b):
                dve.wait_ge(s_stats[kind], at(b, NT, NT))
                mean_e, sq_e, mean_o, sq_o = (stats[:, :, j] for j in (1, 2, 4, 5))
                dve.tensor_tensor(apart[:, :], mean_e, mean_o, ALU.subtract).then_inc(s_join[kind], 1)
                dve.tensor_tensor(mean[kind][:, :], mean_e, mean_o, ALU.add).then_inc(s_join[kind], 1)
                dve.tensor_tensor(var[kind][:, :], sq_e, sq_o, ALU.add).then_inc(s_join[kind], 1)
                dve.wait_ge(s_join[kind], at(b, 4, 3))
                dve.scalar_tensor_tensor(out=apart[:, :], in0=apart[:, :], scalar=0.25, in1=apart[:, :],
                                         op0=ALU.mult, op1=ALU.mult).then_inc(s_join[kind], 1)
                dve.tensor_scalar(mean[kind][:, :], mean[kind][:, :], 0.5, None, ALU.mult).then_inc(s_mv[kind], 1)
                dve.wait_ge(s_join[kind], at(b, 4, 4))
                dve.scalar_tensor_tensor(out=var[kind][:, :], in0=var[kind][:, :], scalar=1.0 / D, in1=apart[:, :],
                                         op0=ALU.mult, op1=ALU.add).then_inc(s_mv[kind], 1)

            def norm_apply(kind, b):
                dve.wait_ge(s_rstd[kind], at(b, 1, 1))
                for t in range(NT):
                    src = h[:, b * NT + t, :] if kind == LOCAL else h2[:, t, :]
                    dve.tensor_scalar(xn[kind][:, t, :], src, mean[kind][:, t:t + 1], rstd[kind][:, t:t + 1],
                                      ALU.subtract, ALU.mult).then_inc(s_xn[kind], 1)

            def copy_x(b):
                for c in range(NC):
                    dve.wait_ge(s_xT_ps[LOCAL], at(b, NC, c + 1))
                    dve.tensor_copy(xT[LOCAL][:, c, :], xT_bank[LOCAL][c]).then_inc(s_xT[LOCAL], 1)

            def leave_rest(kind, b, i):
                dve.wait_ge(s_part1[kind], at(b, 4, i + 1))
                if i >= 2:
                    dve.wait_ge(s_part3[kind], at(b, 4, i - 1))
                dve.scalar_tensor_tensor(out=rest[kind][:, i % 2, :], in0=qk_bank[kind][i],
                                         scalar=qk_bias[kind][:, i % 2, i // 2:i // 2 + 1],
                                         in1=parts[kind][:, i, 0, :], op0=ALU.add, op1=ALU.subtract)\
                    .then_inc(s_rest[kind], 1)

            def store_v(kind, b, j):
                dve.wait_ge(s_v_ps[kind], at(b, 2, j + 1))
                dve.tensor_tensor(VS[kind][:, 2 * j:2 * j + 2, :, 0:HD],
                                  v_bank[kind][j][:, :].rearrange("p (t n d) -> p t n d", t=2, n=H),
                                  v_bias[kind][:, :].rearrange("p (o n d) -> p o n d", o=1, n=H)
                                  .to_broadcast([P, 2, H, HD]), ALU.add).then_inc(s_v[kind], 1)

            def maxima(kind, b, k):
                n = SMAX_TILES[kind]
                head, i = k // n, k % n
                dve.wait_ge(s_sc_ps[kind], at(b, n * H, k + 1))
                if kind == FULL:
                    dve.tensor_reduce(neg_max[FULL][:, i, head:head + 1], SC[k % 2][:, :], AX.X, ALU.max,
                                      negate=True).then_inc(s_max[kind], 1)
                else:
                    dve.tensor_reduce(neg_max[LOCAL][:, 2 * i:2 * i + 2, head],
                                      SC[k % 2][:, :].rearrange("p (w k) -> p w k", w=2), AX.X, ALU.max,
                                      negate=True).then_inc(s_max[kind], 1)
                if (k + 1) % (n * GH) == 0:
                    g = head // GH
                    own = neg_max[kind][:, :, g * GH:(g + 1) * GH]
                    dve.wait_ge(s_max[kind], at(b, n * H, k + 1))
                    if g > 0:
                        dve.wait_ge(s_shT_ps[kind], at(b, G, g))
                    dve.tensor_copy(shift[kind][:, :, 0:GH], own).then_inc(s_sh1[kind], 1)
                    dve.wait_ge(s_sh1[kind], at(b, G, g + 1))
                    dve.tensor_tensor(shift[kind][:, :, GH:2 * GH], own, shift[kind][:, :, 0:GH], ALU.subtract)\
                        .then_inc(s_sh[kind], 1)

            def normalise(kind, b, g):
                dve.wait_ge(s_OT_ps[kind], at(b, G, g + 1))
                o = X[:, :].rearrange("p (t i v) -> p t i v", t=NT, i=GH)
                dve.reciprocal(rden[:, :, :], o[:, :, :, HD]).then_inc(s_rden[kind], 1)
                dve.wait_ge(s_rden[kind], at(b, G, g + 1))
                if kind == FULL and g > 0:
                    dve.wait_ge(s_yadd, at(b, G, g))
                dst = AF[:, :, :] if kind == FULL else AO[:, :, g * GH * HD:(g + 1) * GH * HD]
                for t in range(NT):
                    last = dve.tensor_tensor(dst[:, t, :].rearrange("p (i d) -> p i d", i=GH), o[:, t, :, 0:HD],
                                             rden[:, t, :].unsqueeze(2).to_broadcast([P, GH, HD]), ALU.mult)
                last.then_inc(s_norm[kind], 1)

            def slots(kind, b, more):
                for u in range(UNITS):
                    if u % 4 == (3, 0)[kind] and u >= 7:
                        normalise(kind, b, u // 4 - 1 - kind)
                    for step in ahead_of(kind, b, u, more):
                        maxima(*step)
                    if kind == FULL and u == 0:
                        store_v(FULL, b, 1)
                    if kind == LOCAL and more and u == 9:
                        dve.wait_ge(s_gather, 16 * NT * (B - 1))
                        for t in range(NT):
                            row_stats(LOCAL, b + 1, t)
                        mean_var(LOCAL, b + 1)
                    if kind == LOCAL and more and u == 10:
                        norm_apply(LOCAL, b + 1)
                    if kind == LOCAL and more and u == 13:
                        copy_x(b + 1)
                for g in range(G - 1 - kind, G):
                    normalise(kind, b, g)

            def gate_step(b, ins, k):
                ins.then_inc(s_gs, 1)
                dve.wait_ge(s_gs, at(b, GATE_STEPS, k))

            def gate_logits(b):
                def step(ins, k):
                    gate_step(b, ins, k)

                dve.wait_ge(s_gate_ps, at(b, 1, 1))
                step(dve.tensor_tensor(logit[:, :, :], X[:, 0:NT * E].rearrange("p (t e) -> p t e", t=NT),
                                       gate_bias[:, :].unsqueeze(1).to_broadcast([P, NT, E]), ALU.add), 1)
                step(dve.tensor_reduce(neg_top[:, :], logit[:, :, :], AX.X, ALU.max, negate=True), 2)
                step(dve.tensor_tensor(logit[:, :, :], logit[:, :, :],
                                       neg_top[:, :].unsqueeze(2).to_broadcast([P, NT, E]), ALU.add), 3)

            def gate_weights(b):
                def step(ins, k):
                    gate_step(b, ins, k)

                dve.wait_ge(s_gexp, at(b, 1, 1))
                step(dve.tensor_reduce(gden[:, :], gexp[:, :, :], AX.X, ALU.add), 4)
                dve.reciprocal(grec[:, :], gden[:, :])
                by_e = gexp[:, :, :].unsqueeze(3).to_broadcast([P, NT, E, E])
                by_j = gexp[:, :, :].unsqueeze(2).to_broadcast([P, NT, E, E])
                dve.tensor_tensor(above[:, :, :, :], by_j, by_e, ALU.is_gt)
                step(dve.tensor_tensor(equal[:, :, :, :], by_j, by_e, ALU.is_equal), 5)
                step(dve.tensor_tensor(equal[:, :, :, :], equal[:, :, :, :],
                                       before[:, :, :].unsqueeze(1).to_broadcast([P, NT, E, E]), ALU.mult), 6)
                step(dve.tensor_tensor(above[:, :, :, :], above[:, :, :, :], equal[:, :, :, :], ALU.add), 7)
                step(dve.tensor_reduce(rank[:, :, :], above[:, :, :, :], AX.X, ALU.add), 8)
                step(dve.scalar_tensor_tensor(out=rank[:, :, :], in0=rank[:, :, :], scalar=TOP_K - 0.5,
                                              in1=gexp[:, :, :], op0=ALU.is_lt, op1=ALU.mult), 9)
                dve.tensor_tensor(comb[:, :, :], rank[:, :, :],
                                  grec[:, :].unsqueeze(2).to_broadcast([P, NT, E]), ALU.mult).then_inc(s_comb, 1)

            def add_biases(b, n):
                dve.wait_ge(s_moe, at(b, NT * E, n))
                for j in range(2):
                    dve.wait_ge(s_eb_ps, at(b, 2, j + 1))
                    src = (OB, X)[j][:, :].rearrange("p (t n) -> p t n", t=2)
                    dve.tensor_tensor(y[:, 2 * j:2 * j + 2, :], src, y[:, 2 * j:2 * j + 2, :], ALU.add)\
                        .then_inc(s_yb, 1)

            def add_expert(b, n):
                last_pair = n >= 4 * (PAIRS - 1)
                turn, half = (n % 4 // 2, n % 2) if last_pair else (n % 2, n % 4 // 2)
                s = 2 * (n // 4) + turn
                t, j, bank = expert_bank(s)
                e = 2 * j + half
                if half == 0:
                    dve.wait_ge(s_moe_ps, at(b, NT * E // 2, s + 1))
                if n == 0:
                    dve.wait_ge(s_comb, at(b, 1, 1))
                elif n == 4 * BIAS_PAIR:
                    dve.wait_ge(s_yb, at(b, 2, 2))
                elif n % (2 * E) >= 2:
                    dve.wait_ge(s_moe, at(b, NT * E, n if last_pair and half == 1 else n - 1))
                dve.scalar_tensor_tensor(out=y[:, t, :], in0=ST[:, bank, (e % 2) * D:(e % 2 + 1) * D],
                                         scalar=comb[:, t, e:e + 1], in1=y[:, t, :],
                                         op0=ALU.mult, op1=ALU.add).then_inc(s_moe, 1)

            def row(b, more):
                slots(LOCAL, b, more)
                if more:
                    leave_rest(LOCAL, b + 1, 0)
                    leave_rest(LOCAL, b + 1, 1)
                dve.wait_ge(s_hb, at(b, NT, NT))
                dve.wait_ge(s_out, at(b, 16, 1))
                for j in range(2):
                    dve.wait_ge(s_wo_ps, at(b, 2, j + 1))
                    dve.tensor_tensor(h2[:, 2 * j:2 * j + 2, :],
                                      ST[:, j, :].rearrange("p (t n) -> p t n", t=2),
                                      h[:, bass.ds(b * NT + 2 * j, 2), :], ALU.add).then_inc(s_h2, 1)
                    dve.wait_ge(s_h2, at(b, 2, j + 1))
                    row_stats(FULL, b, 2 * j)
                    row_stats(FULL, b, 2 * j + 1)
                mean_var(FULL, b)
                if more:
                    store_v(LOCAL, b + 1, 0)
                norm_apply(FULL, b)
                if more:
                    leave_rest(LOCAL, b + 1, 2)
                    leave_rest(LOCAL, b + 1, 3)
                    store_v(LOCAL, b + 1, 1)
                gate_logits(b)
                for i in range(4):
                    leave_rest(FULL, b, i)
                gate_weights(b)
                store_v(FULL, b, 0)
                k = 0
                for q in range(PAIRS + 1):
                    if q == BIAS_PAIR + 1:
                        add_biases(b, 4 * (q - 1))
                    adds = range(4 * (q - 1), 4 * q) if q > 0 else range(0)
                    for i in range(max(len(adds), BESIDE[q])):
                        if i < len(adds):
                            add_expert(b, adds[i])
                        if i < BESIDE[q]:
                            maxima(FULL, b, k)
                            k += 1
                slots(FULL, b, more)

            def set_ones(k):
                dve.memset(KS[k][SHIFT_ROW:KROWS, :, :].bitcast(F32), TWO_ONES).then_inc(s_ones, 1)
                dve.memset(VS[k][:, :, :, HD + 1:VW], 0.0).then_inc(s_ones, 1)
                dve.memset(VS[k][:, :, :, HD:HD + 1], 1.0).then_inc(s_ones, 1)

            dve.memset(apart[:, :], 0.0).then_inc(s_out, 1)
            set_ones(LOCAL)
            dve.wait_ge(s_first, 16 * NT)
            for t in range(NT):
                row_stats(LOCAL, 0, t)
            mean_var(LOCAL, 0)
            norm_apply(LOCAL, 0)
            copy_x(0)
            dve.wait_ge(s_w, 16 * QK_LOADS)
            for i in range(4):
                leave_rest(LOCAL, 0, i)
            for j in range(2):
                store_v(LOCAL, 0, j)
            set_ones(FULL)
            for k in range(LEAD[LOCAL] * SMAX_TILES[LOCAL]):
                maxima(LOCAL, 0, k)
            dve.wait_ge(s_w2, 16 * OTHER_LOADS)
            with dve.Fori(0, B - 1) as b:
                row(b, True)
            row(B - 1, False)

        @block.tensor
        def _(pe):
            def keep_warm(n):
                for _ in range(n):
                    pe.matmul(OB[:, 0:D], ident[:, :], w_q[:, 0, :], start=True, stop=True)

            def turn_x(kind, b):
                for t in range(NT):
                    pe.wait_ge(s_xn[kind], at(b, NT, t + 1))
                    for c in range(NC):
                        mm = pe.transpose(xT_bank[kind][c][:, t * P:(t + 1) * P], xn[kind][:, t, c * P:(c + 1) * P],
                                          ident[:, :])
                        if t == NT - 1:
                            mm.then_inc(s_xT_ps[kind], 1)

            def project_qk(kind, b, i):
                pe.wait_ge(s_xT[kind], at(b, NC, NC))
                j, m = i % 2, i // 2
                for c in range(NC):
                    w = (w_q, w_k)[j][:, c, m * P:(m + 1) * P] if kind == LOCAL else \
                        w_qkv[:, c, j * D + m * P:j * D + (m + 1) * P]
                    mm = pe.matmul(qk_bank[kind][i], w, xT[kind][:, c, :], start=(c == 0), stop=(c == NC - 1))
                mm.then_inc(s_qk_ps[kind], 1)

            def project_v(kind, b, j):
                if kind == LOCAL:
                    pe.wait_ge(s_rest[LOCAL], at(b, 4, j + 1))
                for t in (2 * j, 2 * j + 1):
                    for c in range(NC):
                        w = w_v[:, c, :] if kind == LOCAL else w_qkv[:, c, 2 * D:3 * D]
                        mm = pe.matmul(v_bank[kind][j][:, (t % 2) * D:(t % 2 + 1) * D], xT[kind][:, c, t * P:(t + 1) * P], w,
                                       start=(c == 0), stop=(c == NC - 1))
                mm.then_inc(s_v_ps[kind], 1)

            def row_scores(kind, b, k):
                n = SMAX_TILES[kind]
                head, i = k // n, k % n
                if k >= 2:
                    pe.wait_ge(s_max[kind], at(b, n * H, k - 1))
                elif kind == FULL:
                    pe.wait_ge(s_v[FULL], at(b, 2, 1))
                elif isinstance(b, int) and b == 0:
                    pe.wait_ge(s_v[LOCAL], 2)
                else:
                    pe.wait_ge(s_max[FULL], at(b - 1, 4 * H, 4 * H))
                if head % 8 == 0 and i == 0:
                    pe.wait_ge(s_stacked[head // 8][kind], at(b, STACK_LOADS, STACK_LOADS))
                bank = SC[k % 2]
                if kind == FULL:
                    pe.matmul(bank[:, :], QS[FULL][0:SHIFT_ROW, head, i * P:(i + 1) * P], KS[FULL][0:SHIFT_ROW, head, :],
                              start=True, stop=True).then_inc(s_sc_ps[FULL], 1)
                    return
                for w in (2 * i, 2 * i + 1):
                    q = QS[LOCAL][0:SHIFT_ROW, head, w * P:(w + 1) * P]
                    o = (w % 2) * 2 * P
                    if w > 0:
                        pe.matmul(bank[:, o:o + 2 * P], q, KS[LOCAL][0:SHIFT_ROW, head, (w - 1) * P:(w + 1) * P],
                                  start=(w % 2 == 0), stop=False, skip_group_check=True)
                    else:
                        for j in range(2):
                            pe.matmul(bank[:, j * P:(j + 1) * P], q, KS[LOCAL][0:SHIFT_ROW, head, 0:P],
                                      start=(j == 0), stop=False, skip_group_check=True)
                        pe.matmul(bank[:, 0:P], ident_bf[:, :], mask_q[:, :], start=False, stop=False,
                                  skip_group_check=True)
                    mm = pe.matmul(bank[:, o + P:o + 2 * P], ident_bf[:, :], mask_q[:, :], start=False,
                                   stop=(w % 2 == 1), skip_group_check=True)
                mm.then_inc(s_sc_ps[LOCAL], 1)

            def turn_shift(kind, b, g):
                pe.wait_ge(s_sh[kind], at(b, G, g + 1))
                for t in range(NT):
                    mm = pe.transpose(X_bf[0:2 * GH, t * P:(t + 1) * P], shift[kind][:, t, :], ident_bf[:, :])
                mm.then_inc(s_shT_ps[kind], 1)

            def scores(kind, b, u, e):
                g, kt = u // NT, u % NT
                if kt == 0 and e == 0:
                    pe.wait_ge(s_shrow[kind], at(b, 32 * G, 32 * (g + 1)))
                keys = slice(kt * P, (kt + 1) * P)
                if kind == FULL:
                    if u > 0:
                        pe.wait_ge(s_prob[FULL], at(b, 2 * UNITS, 2 * (u - 1) + e + 1))
                    else:
                        pe.wait_ge(s_moe, at(b, NT * E, NT * E - 4 + 4 * e))
                    for i in (2 * e, 2 * e + 1):
                        head = g * GH + i
                        mm = pe.matmul(ST[:, i, :], KS[FULL][0:KROWS, head, keys], QS[FULL][0:KROWS, head, :],
                                       start=True, stop=True)
                    mm.then_inc(s_st_ps[FULL], 1)
                    return
                if u >= 2:
                    pe.wait_ge(s_prob[LOCAL], at(b, UNITS, u - 1))
                w = 2 * P if kt < NT - 1 else P
                for i in range(GH):
                    head = g * GH + i
                    bank = ST_local[:, 4 * (u % 2) + i, :]
                    pe.matmul(bank[:, 0:w], KS[LOCAL][0:KROWS, head, keys], QS[LOCAL][0:KROWS, head, kt * P:kt * P + w],
                              start=(i % 2 == 0), stop=False, skip_group_check=True)
                    mm = pe.matmul(bank[:, 0:P], ident_bf[:, :], mask_k[:, :], start=False, stop=(i % 2 == 1),
                                   skip_group_check=True)
                mm.then_inc(s_st_ps[LOCAL], 1)

            def times_v(kind, b, u, half=0):
                g, kt = u // NT, u % NT
                pe.wait_ge(s_prob[kind], at(b, EXPS[kind] * UNITS, EXPS[kind] * (u + 1)))
                if u in (0, 2):
                    pe.wait_ge(s_v[kind], at(b, 2, u // 2 + 1))
                if kt == 0:
                    if g > 0:
                        pe.wait_ge(s_OT[kind], at(b, G, g))
                    elif kind == FULL:
                        pe.wait_ge(s_yb, at(b, 2, 1))
                w = 2 * P if kt < NT - 1 else P
                columns = slice(half * 2 * P, (half + 1) * 2 * P) if kind == FULL else slice(kt * P, kt * P + w)
                source = columns if kind == FULL else slice(0, w)
                for i in range(GH):
                    mm = pe.matmul(OB[VW * i:VW * (i + 1), columns], VS[kind][:, kt, g * GH + i, :],
                                   prob[:, u % 2, i, source], start=(kt == 0 and half == 0),
                                   stop=(kt == NT - 1), skip_group_check=True)
                if kind == LOCAL or half == 1:
                    mm.then_inc(s_pv[kind], 1)

            def turn_O(kind, b, g):
                pe.wait_ge(s_OT[kind], at(b, G, g + 1))
                for t in range(NT):
                    mm = pe.transpose(X[:, t * P:(t + 1) * P], OT[:, t * P:(t + 1) * P], ident[:, :])
                mm.then_inc(s_OT_ps[kind], 1)

            def next_shift(kind, b, u):
                if u % 4 == 1 + kind and u < 12:
                    pe.wait_ge(s_shT[kind], at(b, G, u // 4 + 1))
                    if u // 4 == 2:
                        pe.wait_ge(s_norm[kind], at(b, G, 1))
                    elif kind == FULL and u // 4 == 0:
                        pe.wait_ge(s_v[FULL], at(b, 2, 2))
                    turn_shift(kind, b, u // 4 + 1)

            def slots(kind, b, more):
                for u in range(UNITS):
                    ahead = ahead_of(kind, b, u, more)
                    quarters = [ahead[i * len(ahead) // 4:(i + 1) * len(ahead) // 4] for i in range(4)]
                    if kind == FULL:
                        scores(kind, b, u, 0)
                        for step in quarters[0]:
                            row_scores(*step)
                        scores(kind, b, u, 1)
                        for step in quarters[1]:
                            row_scores(*step)
                    else:
                        if u > 0:
                            scores(kind, b, u, 0)
                        for step in quarters[0] + quarters[1]:
                            row_scores(*step)
                    if u == 14 and kind == FULL and more:
                        pe.wait_ge(s_norm[FULL], at(b, G, 2))
                        turn_shift(LOCAL, b + 1, 0)
                    if u == 15 and kind == FULL:
                        turn_O_in(kind, b, u, more)
                    if kind == FULL:
                        next_shift(kind, b, u)
                    if u > 0:
                        times_v(kind, b, u - 1)
                    if kind == LOCAL:
                        next_shift(kind, b, u)
                    for step in quarters[2]:
                        row_scores(*step)
                    if u > 0 and kind == FULL:
                        times_v(kind, b, u - 1, 1)
                    for step in quarters[3]:
                        row_scores(*step)
                    if u % 4 == 2 + kind and 5 < u < 15:
                        turn_O_in(kind, b, u, more)
                    if kind == LOCAL and more and u == 12:
                        turn_x(LOCAL, b + 1)
                    if kind == LOCAL and more and u == 14:
                        project_qk(LOCAL, b + 1, 0)
                for half in range(1 + kind):
                    times_v(kind, b, UNITS - 1, half)

            def turn_O_in(kind, b, u, more):
                if u < 12:
                    pe.wait_ge(s_shT[kind], at(b, G, u // 4 + 2))
                elif kind == FULL and more:
                    pe.wait_ge(s_shT[LOCAL], at(b + 1, G, 1))
                else:
                    pe.wait_ge(s_norm[kind], at(b, G, 2))
                turn_O(kind, b, u // 4 - 1)

            def last_group(kind, b):
                pe.wait_ge(s_norm[kind], at(b, G, G - 1))
                turn_O(kind, b, G - 1)

            def turn_AO(b, c):
                pe.wait_ge(s_norm[LOCAL], at(b, G, 2 * (c + 1)))
                for t in range(NT):
                    mm = pe.transpose(ST[:, c, t * P:(t + 1) * P], AO[:, t, c * P:(c + 1) * P], ident[:, :])
                mm.then_inc(s_ao_ps, 1)

            def two_experts(b, s, c):
                t, j, bank = expert_bank(s)
                if c == 0 and s == 0:
                    pe.wait_ge(s_rest[FULL], at(b, 4, 4))
                elif c == 0 and s >= 4:
                    pe.wait_ge(s_moe, at(b, NT * E, 4 * (s // 2 - 2) + 3 + s % 2))
                mm = pe.matmul(ST[:, bank, :], xT[FULL][:, c, t * P:(t + 1) * P], w_exp[:, c, 2 * j:2 * j + 2, :],
                               start=(c == 0), stop=(c == NC - 1))
                if c == NC - 1:
                    mm.then_inc(s_moe_ps, 1)

            def row(b, more):
                slots(LOCAL, b, more)
                turn_AO(b, 0)
                last_group(LOCAL, b)
                if more:
                    project_qk(LOCAL, b + 1, 1)
                turn_AO(b, 1)
                if more:
                    project_qk(LOCAL, b + 1, 2)
                pe.wait_ge(s_ao, at(b, NC, NC))
                for j in range(2):
                    for t in (2 * j, 2 * j + 1):
                        for c in range(NC):
                            mm = pe.matmul(ST[:, j, (t % 2) * D:(t % 2 + 1) * D], AOT[:, c, t * P:(t + 1) * P],
                                           w_o[:, c, :], start=(c == 0), stop=(c == NC - 1))
                    mm.then_inc(s_wo_ps, 1)
                if more:
                    project_v(LOCAL, b + 1, 0)
                    project_qk(LOCAL, b + 1, 3)
                else:
                    keep_warm(WARM[2])
                turn_x(FULL, b)
                if more:
                    project_v(LOCAL, b + 1, 1)
                pe.wait_ge(s_xT[FULL], at(b, NC, NC))
                for t in range(NT):
                    for c in range(NC):
                        mm = pe.matmul(X[:, t * E:(t + 1) * E], xT[FULL][:, c, t * P:(t + 1) * P], w_gate[:, c, :],
                                       start=(c == 0), stop=(c == NC - 1))
                mm.then_inc(s_gate_ps, 1)
                if more:
                    pe.wait_ge(s_rest[LOCAL], at(b + 1, 4, 4))
                for i in range(4):
                    project_qk(FULL, b, i)
                if more:
                    pe.wait_ge(s_v[LOCAL], at(b + 1, 2, 2))
                project_v(FULL, b, 0)
                k = 0
                for q in range(PAIRS + 1):
                    for i in range(4):
                        if q < PAIRS:
                            two_experts(b, 2 * q + i // 2, i % 2)
                        for _ in range(BESIDE[q] * i // 4, BESIDE[q] * (i + 1) // 4):
                            row_scores(FULL, b, k)
                            k += 1
                            if k == GH * SMAX_TILES[FULL] + FIRST_SHIFT:
                                pe.wait_ge(s_yb, at(b, 2, 2))
                                turn_shift(FULL, b, 0)
                    if q == BIAS_PAIR - 1:
                        pe.wait_ge(s_comb, at(b, 1, 1))
                        for t in range(NT):
                            mm = pe.transpose(X[0:E, t * P:(t + 1) * P], comb[:, t, :], ident[:, :])
                        mm.then_inc(s_comb_ps, 1)
                    if q == BIAS_PAIR:
                        pe.wait_ge(s_combT, at(b, 1, 1))
                        for j in range(2):
                            for t in (2 * j, 2 * j + 1):
                                mm = pe.matmul((OB, X)[j][:, (t % 2) * D:(t % 2 + 1) * D],
                                               combT[:, t * P:(t + 1) * P], exp_bias[:, :], start=True, stop=True)
                            mm.then_inc(s_eb_ps, 1)
                pe.wait_ge(s_shT[FULL], at(b, G, 1))
                project_v(FULL, b, 1)
                slots(FULL, b, more)
                if more:
                    scores(LOCAL, b + 1, 0, 0)
                last_group(FULL, b)

            pe.wait_ge(s_const, 5)
            pe.wait_ge(s_w, 16 * QK_LOADS)
            keep_warm(WARM[0])
            turn_x(LOCAL, 0)
            for i in range(4):
                project_qk(LOCAL, 0, i)
            for j in range(2):
                project_v(LOCAL, 0, j)
            keep_warm(WARM[1])
            for k in range(LEAD[LOCAL] * SMAX_TILES[LOCAL]):
                row_scores(LOCAL, 0, k)
                if k + 1 == GH * SMAX_TILES[LOCAL] + FIRST_SHIFT:
                    turn_shift(LOCAL, 0, 0)
            pe.wait_ge(s_rest[LOCAL], 4)
            pe.wait_ge(s_ones, 6)
            pe.wait_ge(s_w2, 16 * OTHER_LOADS)
            scores(LOCAL, 0, 0, 0)
            with pe.Fori(0, B - 1) as b:
                row(b, True)
            row(B - 1, False)


_INS = ['x', 'L0_tok_W', 'L0_attn_Wq', 'L0_attn_bq', 'L0_attn_Wk', 'L0_attn_bk', 'L0_attn_Wv', 'L0_attn_bv',
        'L0_attn_Wo', 'L0_attn_bo', 'L0_ffn_W_qkv', 'L0_ffn_b_qkv', 'L0_ffn_W_gate', 'L0_ffn_b_gate',
        'L0_ffn_W_experts', 'L0_ffn_b_experts']


def kernel(**inputs):
    import concourse.bacc as bacc
    from concourse.bass_utils import run_bass_kernel_spmd

    nc = bacc.Bacc("TRN2", target_bir_lowering=False, num_devices=1)
    arrays, args = {}, []
    for name in _INS:
        a = np.asarray(inputs[name])
        if name == 'x':
            a = a.reshape(B * NT, P).T
        a = np.ascontiguousarray(a)
        arrays[f"in_{name}"] = a
        args.append(nc.dram_tensor(f"in_{name}", a.shape, mybir.dt.from_np(a.dtype), kind="ExternalInput").ap())
    out = nc.dram_tensor("out", (B, T, D), F32, kind="ExternalOutput").ap()
    tower(nc, *args, out)
    result = run_bass_kernel_spmd(nc, [arrays], core_ids=[0])
    return result.results[0]["out"]
```
